# Optimizing a Trainium2 kernel written in Bass

```python
import numpy as np
import jax
import jax.numpy as jnp

def _softmax(x, axis=-1):
    return jax.nn.softmax(x, axis=axis)

def _gelu(x):
    return jax.nn.gelu(x, approximate=True)

def _silu(x):
    return jax.nn.silu(x)

def _sigmoid(x):
    return jax.nn.sigmoid(x)

def _layernorm(x, axis=-1, eps=1e-05):
    m = jnp.mean(x, axis=axis, keepdims=True)
    v = jnp.var(x, axis=axis, keepdims=True)
    return (x - m) / jnp.sqrt(v + eps)

def _scatter_add(tgt, idx, src, axis=0):
    return tgt.at[idx].add(src)

def _segment_sum(src, seg, n):
    return jax.ops.segment_sum(src, seg, n)
kernel_name = 'mk_vit_tower_d1_tok_img768_r4_277655'

def setup_inputs(seed: int=0):
    np.random.seed(seed)
    _w = jnp.asarray

    def _rec_inputs():
        import jax
        import jax.numpy as jnp
        _rk = jax.random.key(seed)
        x = -0.000356955 + 1 * jax.random.normal(jax.random.fold_in(_rk, 1), (64, 3, 96, 96), jnp.float32)
        return x
    x = _rec_inputs()

    def _L0_tok_setup():
        import jax, jax.numpy as jnp
        import numpy as np
        IMAGE_SIZE = 224
        PATCH = 16
        HIDDEN = 192
        C = 3
        key = jax.random.key(seed)
        k1, k2, k3 = jax.random.split(key, 3)
        img = jax.random.normal(k1, (128, C, IMAGE_SIZE, IMAGE_SIZE), dtype=jnp.float32)
        d_in = C * PATCH * PATCH
        bound = 1.0 / np.sqrt(d_in)
        W = jax.random.uniform(k2, (HIDDEN, d_in), jnp.float32, -bound, bound)
        b = jax.random.uniform(k3, (HIDDEN,), jnp.float32, -bound, bound)
        return {'img': img, 'W': W, 'b': b}
    _L0_tok_all = _L0_tok_setup()
    _L0_tok_in = {k: v for k, v in _L0_tok_all.items() if k in ('W', 'b')}
    del _L0_tok_all

    def _L0_attn_setup():
        import jax, jax.numpy as jnp
        import numpy as np
        D_MODEL = 192
        N_HEAD = 12
        D_HEAD = D_MODEL // N_HEAD
        N_CTX = 512
        ROPE_BASE = float(N_CTX)
        SCALE = 1
        EPS = 1e-06

        def _rope_tables(seq_len):
            inv_freq = 1.0 / ROPE_BASE ** (jnp.arange(0, D_HEAD, 2, dtype=jnp.float32) / D_HEAD)
            t = jnp.arange(seq_len, dtype=jnp.float32)
            freqs = jnp.outer(t, inv_freq)
            return (jnp.cos(freqs), jnp.sin(freqs))

        def _rmsnorm(x, g):
            return x * jax.lax.rsqrt(jnp.mean(x * x, axis=-1, keepdims=True) + EPS) * g

        def _apply_rope(x, cos, sin):
            d = D_HEAD // 2
            x1, x2 = (x[..., :d], x[..., d:])
            c = cos[None, :, None, :]
            s = sin[None, :, None, :]
            return jnp.concatenate([x1 * c + x2 * s, -x1 * s + x2 * c], axis=-1)
        key = jax.random.key(seed)
        ks = jax.random.split(key, 10)
        sd = 1.0 / np.sqrt(D_MODEL)
        x = jax.random.normal(ks[0], (2, N_CTX, D_MODEL), jnp.float32)
        Wq = jax.random.uniform(ks[1], (D_MODEL, D_MODEL), jnp.float32, -sd, sd)
        bq = jax.random.uniform(ks[2], (D_MODEL,), jnp.float32, -sd, sd)
        Wk = jax.random.uniform(ks[3], (D_MODEL, D_MODEL), jnp.float32, -sd, sd)
        bk = jax.random.uniform(ks[4], (D_MODEL,), jnp.float32, -sd, sd)
        Wv = jax.random.uniform(ks[5], (D_MODEL, D_MODEL), jnp.float32, -sd, sd)
        bv = jax.random.uniform(ks[6], (D_MODEL,), jnp.float32, -sd, sd)
        Wo = jax.random.uniform(ks[7], (D_MODEL, D_MODEL), jnp.float32, -sd, sd)
        g = 1.0 + 0.1 * jax.random.normal(ks[8], (D_HEAD,), jnp.float32)
        return {'x': x, 'Wq': Wq, 'bq': bq, 'Wk': Wk, 'bk': bk, 'Wv': Wv, 'bv': bv, 'Wo': Wo, 'g': g}
    _L0_attn_all = _L0_attn_setup()
    _L0_attn_in = {k: v for k, v in _L0_attn_all.items() if k in ('Wq', 'bq', 'Wk', 'bk', 'Wv', 'bv', 'Wo', 'g')}
    del _L0_attn_all

    def _L0_ffn_setup():
        import jax, jax.numpy as jnp
        import numpy as np
        DIM = 192
        NUM_HEADS = 12
        HEAD_DIM = DIM // NUM_HEADS
        SCALE = HEAD_DIM ** (-0.5)
        NUM_EXPERTS = 8
        RANK = 16
        ALPHA = 32
        TOPK = 2
        SCALING = ALPHA / RANK
        B, S = (8, 256)
        key = jax.random.key(seed)
        ks = jax.random.split(key, 12)
        d, e, r = (DIM, NUM_EXPERTS, RANK)
        inp = {'x': jax.random.normal(ks[0], (B, S, d), jnp.float32), 'Wg': jax.random.normal(ks[1], (e, d), jnp.float32) * 0.02, 'bg': jax.random.normal(ks[2], (e,), jnp.float32) * 0.02, 'Wqkv': jax.random.normal(ks[3], (3 * d, d), jnp.float32) * 0.02, 'bqkv': jax.random.normal(ks[4], (3 * d,), jnp.float32) * 0.02, 'Wproj': jax.random.normal(ks[5], (d, d), jnp.float32) * 0.02, 'bproj': jax.random.normal(ks[6], (d,), jnp.float32) * 0.02, 'A': jax.random.normal(ks[7], (e, r, d), jnp.float32) * 0.05, 'ba': jax.random.normal(ks[8], (e, r), jnp.float32) * 0.02, 'Bm': jax.random.normal(ks[9], (e, 3 * d, r), jnp.float32) * 0.05, 'bb': jax.random.normal(ks[10], (e, 3 * d), jnp.float32) * 0.02}
        return inp
    _L0_ffn_all = _L0_ffn_setup()
    _L0_ffn_in = {k: v for k, v in _L0_ffn_all.items() if k in ('Wg', 'bg', 'Wqkv', 'bqkv', 'Wproj', 'bproj', 'A', 'ba', 'Bm', 'bb')}
    del _L0_ffn_all
    return {'x': x, 'L0_tok_W': _L0_tok_in['W'], 'L0_tok_b': _L0_tok_in['b'], 'L0_attn_Wq': _L0_attn_in['Wq'], 'L0_attn_bq': _L0_attn_in['bq'], 'L0_attn_Wk': _L0_attn_in['Wk'], 'L0_attn_bk': _L0_attn_in['bk'], 'L0_attn_Wv': _L0_attn_in['Wv'], 'L0_attn_bv': _L0_attn_in['bv'], 'L0_attn_Wo': _L0_attn_in['Wo'], 'L0_attn_g': _L0_attn_in['g'], 'L0_ffn_Wg': _L0_ffn_in['Wg'], 'L0_ffn_bg': _L0_ffn_in['bg'], 'L0_ffn_Wqkv': _L0_ffn_in['Wqkv'], 'L0_ffn_bqkv': _L0_ffn_in['bqkv'], 'L0_ffn_Wproj': _L0_ffn_in['Wproj'], 'L0_ffn_bproj': _L0_ffn_in['bproj'], 'L0_ffn_A': _L0_ffn_in['A'], 'L0_ffn_ba': _L0_ffn_in['ba'], 'L0_ffn_Bm': _L0_ffn_in['Bm'], 'L0_ffn_bb': _L0_ffn_in['bb']}

def reference(x, L0_tok_W, L0_tok_b, L0_attn_Wq, L0_attn_bq, L0_attn_Wk, L0_attn_bk, L0_attn_Wv, L0_attn_bv, L0_attn_Wo, L0_attn_g, L0_ffn_Wg, L0_ffn_bg, L0_ffn_Wqkv, L0_ffn_bqkv, L0_ffn_Wproj, L0_ffn_bproj, L0_ffn_A, L0_ffn_ba, L0_ffn_Bm, L0_ffn_bb):
    import jax
    import jax.numpy as jnp

    def _L0_tok_ref(img, W, b):
        import jax, jax.numpy as jnp
        import numpy as np
        IMAGE_SIZE = 224
        PATCH = 16
        HIDDEN = 192
        C = 3
        B, Cc, H, Wd = img.shape
        hp, wp = (H // PATCH, W // PATCH if False else Wd // PATCH)
        hp = H // PATCH
        x = img.reshape(B, Cc, hp, PATCH, wp, PATCH)
        x = x.transpose(0, 2, 4, 1, 3, 5)
        x = x.reshape(B, hp * wp, Cc * PATCH * PATCH)
        return jnp.einsum('bld,hd->blh', x, W) + b

    def _L0_attn_ref(x, Wq, bq, Wk, bk, Wv, bv, Wo, g):
        import jax, jax.numpy as jnp
        import numpy as np
        D_MODEL = 192
        N_HEAD = 12
        D_HEAD = D_MODEL // N_HEAD
        N_CTX = 512
        ROPE_BASE = float(N_CTX)
        SCALE = 1
        EPS = 1e-06

        def _rope_tables(seq_len):
            inv_freq = 1.0 / ROPE_BASE ** (jnp.arange(0, D_HEAD, 2, dtype=jnp.float32) / D_HEAD)
            t = jnp.arange(seq_len, dtype=jnp.float32)
            freqs = jnp.outer(t, inv_freq)
            return (jnp.cos(freqs), jnp.sin(freqs))

        def _rmsnorm(x, g):
            return x * jax.lax.rsqrt(jnp.mean(x * x, axis=-1, keepdims=True) + EPS) * g

        def _apply_rope(x, cos, sin):
            d = D_HEAD // 2
            x1, x2 = (x[..., :d], x[..., d:])
            c = cos[None, :, None, :]
            s = sin[None, :, None, :]
            return jnp.concatenate([x1 * c + x2 * s, -x1 * s + x2 * c], axis=-1)
        B, S, _ = x.shape
        q = (x @ Wq.T + bq).reshape(B, S, N_HEAD, D_HEAD)
        k = (x @ Wk.T + bk).reshape(B, S, N_HEAD, D_HEAD)
        v = (x @ Wv.T + bv).reshape(B, S, N_HEAD, D_HEAD)
        cos, sin = _rope_tables(S)
        q = _apply_rope(_rmsnorm(q, g), cos, sin)
        k = _apply_rope(_rmsnorm(k, g), cos, sin)
        scores = jnp.einsum('bqhd,bkhd->bhqk', q, k)
        causal = jnp.tril(jnp.ones((S, S), dtype=x.dtype))
        pattern = jnp.square(scores / D_HEAD) * causal
        z = jnp.einsum('bhqk,bkhd->bqhd', pattern, v).reshape(B, S, D_MODEL)
        return z @ Wo.T * SCALE

    def _L0_ffn_ref(x, Wg, bg, Wqkv, bqkv, Wproj, bproj, A, ba, Bm, bb):
        import jax, jax.numpy as jnp
        import numpy as np
        DIM = 192
        NUM_HEADS = 12
        HEAD_DIM = DIM // NUM_HEADS
        SCALE = HEAD_DIM ** (-0.5)
        NUM_EXPERTS = 8
        RANK = 16
        ALPHA = 32
        TOPK = 2
        SCALING = ALPHA / RANK
        B, S = (8, 256)
        b, s, d = x.shape
        t = b * s
        xf = x.reshape(t, d)
        probs = jax.nn.softmax(xf @ Wg.T + bg, axis=-1)
        top_w, top_idx = jax.lax.top_k(probs, TOPK)
        combine = jnp.zeros((t, NUM_EXPERTS), x.dtype).at[jnp.arange(t)[:, None], top_idx].add(top_w)
        h = jnp.einsum('td,erd->ter', xf, A) + ba
        hw = h * combine[:, :, None]
        delta = jnp.einsum('ter,eor->to', hw, Bm) + combine @ bb
        delta = delta * SCALING
        qkv = xf @ Wqkv.T + bqkv + delta
        qkv = qkv.reshape(b, s, 3, NUM_HEADS, HEAD_DIM)
        qkv = jnp.transpose(qkv, (2, 0, 3, 1, 4))
        q, k, v = (qkv[0], qkv[1], qkv[2])
        attn = jax.nn.softmax(jnp.einsum('bhsd,bhtd->bhst', q, k) * SCALE, axis=-1)
        out = jnp.einsum('bhst,bhtd->bhsd', attn, v)
        out = jnp.transpose(out, (0, 2, 1, 3)).reshape(b, s, d)
        return out @ Wproj.T + bproj
    h = _L0_tok_ref(x, L0_tok_W, L0_tok_b)
    h = h + _L0_attn_ref(_layernorm(h, axis=-1), L0_attn_Wq, L0_attn_bq, L0_attn_Wk, L0_attn_bk, L0_attn_Wv, L0_attn_bv, L0_attn_Wo, L0_attn_g)
    h = h + _L0_ffn_ref(_layernorm(h, axis=-1), L0_ffn_Wg, L0_ffn_bg, L0_ffn_Wqkv, L0_ffn_bqkv, L0_ffn_Wproj, L0_ffn_bproj, L0_ffn_A, L0_ffn_ba, L0_ffn_Bm, L0_ffn_bb)
    return h

_drawn_inputs = setup_inputs


def setup_inputs(seed=0):
    import zlib

    import numpy as np

    out = dict(_drawn_inputs(seed))
    spreads = {}
    factors = {'L0_attn_bq': 2.869,
     'L0_attn_bk': 2.908,
     'L0_ffn_Wg': 8.0,
     'L0_ffn_bg': 8.0,
     'L0_ffn_bqkv': 6.944,
     'L0_ffn_A': 8.0,
     'L0_ffn_ba': 8.0,
     'L0_ffn_Bm': 8.0,
     'L0_ffn_bb': 8.0,
     'L0_ffn_bproj': 8.0}
    for name, (base, spread) in spreads.items():
        noise = np.random.default_rng([zlib.crc32(name.encode()), seed]).standard_normal(out[name].shape)
        drawn = base * np.exp(spread * noise) if base else spread * noise
        out[name] = jnp.asarray(drawn.astype(out[name].dtype))
    for name, factor in factors.items():
        out[name] = (out[name] * factor).astype(out[name].dtype)
    return out
```

```python
import concourse.bass as bass
from concourse import mybir
from contextlib import ExitStack


def vit_tower(nc, x_tiles, w_tok, b_tok, w_qkv1, w_o1, g_rows, rope_rows, causal_keep,
              w_gate, w_qkv2, w_lora, w_proj, b_proj, image_rows, identity, out):
    fp32 = mybir.dt.float32
    ALU = mybir.AluOpType
    ACT = mybir.ActivationFunctionType
    AX = mybir.AxisListType

    TILES, P, CK, T = x_tiles.shape
    D = w_tok.shape[2]
    H = 12
    DH = D // H
    HALF = DH // 2
    D2 = D - P
    HG = 3
    HPG = H // HG
    SLOT = P // HPG
    ROUNDS = HPG
    HR = HG
    E = 8
    R = w_lora.shape[0]
    RANK = R // E
    KX = DH + 3
    LN_EPS = 1e-5
    RMS_EPS = 1e-6
    LORA_SCALE = 2.0
    SM_SCALE = DH ** -0.5
    STAGES = 4

    with ExitStack() as ctx:
        def sb(name, shape):
            return ctx.enter_context(nc.sbuf_tensor(name, shape, fp32))

        def bank(name):
            return ctx.enter_context(nc.psum_tensor(name, [P, 512], fp32))

        def sem(name):
            return ctx.enter_context(nc.semaphore(name))

        tok_w = sb("tok_w", [P, CK, D])
        tok_b = sb("tok_b", [T, D])
        qkv1_w0 = sb("qkv1_w0", [P, 3 * D])
        qkv1_w1 = sb("qkv1_w1", [D2 + 1, 3 * D])
        o1_w0 = sb("o1_w0", [P, D])
        o1_w1 = sb("o1_w1", [D2, D])
        gate_w0 = sb("gate_w0", [P, R + E])
        gate_w1 = sb("gate_w1", [D2 + 1, R + E])
        qkv2_w0 = sb("qkv2_w0", [P, 3 * D])
        qkv2_w1 = sb("qkv2_w1", [D2 + 1 + E, 3 * D])
        lora_w = sb("lora_w", [R, 3 * D])
        proj_w0 = sb("proj_w0", [P, D])
        proj_w1 = sb("proj_w1", [D2, D])
        proj_b = sb("proj_b", [T, D])
        ident = sb("ident", [P, P])
        keep = sb("keep", [T, T])
        g_sb = sb("g_sb", [T, 2 * DH])
        rope_sb = sb("rope_sb", [T, 2 * DH])
        rope = sb("rope", [T, 2 * DH])
        minus_half = sb("minus_half", [T, 2 * H])

        x_sb = [sb(f"x_sb{i}", [P, CK, T]) for i in range(2)]
        out_sb = [sb(f"out_sb{i}", [T, D]) for i in range(2)]
        h0 = [sb(f"h0_{i}", [T, D]) for i in range(2)]
        qk1 = [sb(f"qk1_{i}", [T, 2 * H, DH]) for i in range(2)]
        v1 = [sb(f"v1_{i}", [T, D]) for i in range(2)]
        h1 = [sb(f"h1_{i}", [T, D]) for i in range(2)]
        h1b = [sb(f"h1b_{i}", [T, D]) for i in range(2)]
        v2 = [sb(f"v2_{i}", [T, H, DH + 1]) for i in range(2)]

        stat0 = sb("stat0", [T, 6])
        mv0 = sb("mv0", [T, 2])
        var0 = sb("var0", [T, 1])
        rstd0 = sb("rstd0", [T, 1])
        xn = sb("xn", [T, 2 * P])
        xnT = sb("xnT", [P, 2, T])
        sq = sb("sq", [T, 2 * H, DH])
        ss = sb("ss", [T, 2 * H])
        ms = sb("ms", [T, 2 * H])
        rms = sb("rms", [T, 2 * H])
        qkn = sb("qkn", [T, 2 * H, DH])
        own = sb("own", [T, 2 * H, DH])
        other = sb("other", [T, 2 * H, DH])
        slot1 = sb("slot1", [T, 2 * H, SLOT])
        qk1T = sb("qk1T", [P, 2, HG, T])
        pat = sb("pat", [T, H, T])
        z1 = sb("z1", [T, D])
        z1T = sb("z1T", [P, 2, T])
        stat1 = sb("stat1", [T, 6])
        mv1 = sb("mv1", [T, 2])
        var1 = sb("var1", [T, 1])
        rstd1 = sb("rstd1", [T, 1])
        xc = sb("xc", [T, 2 * P])
        x2T = sb("x2T", [P, 2, T])
        nmax = sb("nmax", [T, 1])
        ex = sb("ex", [T, 2 * E])
        exsum = sb("exsum", [T, 1])
        rsum = sb("rsum", [T, 1])
        lora_scale = sb("lora_scale", [T, 1])
        top = sb("top", [T, E])
        top2 = sb("top2", [T, E])
        rest = sb("rest", [T, 2 * E])
        picked = sb("picked", [T, E])
        hw = sb("hw", [T, E, RANK])
        catT = sb("catT", [P, 2, T])
        slot2 = sb("slot2", [T, 2 * H, SLOT])
        qk2T = sb("qk2T", [P, 2, HG, T])
        smax = sb("smax", [T, H])
        prob = sb("prob", [T, H, T])
        probT = sb("probT", [T, H, T])
        rden = sb("rden", [T, H])
        z2 = sb("z2", [T, H, DH])
        z2T = sb("z2T", [P, 2, T])

        banks = [bank(f"bank{i}") for i in range(8)]

        ps_tok = banks[0][0:T, 0:D]
        ps_xnT = banks[0][:, D:D + 2 * T]
        ps_qk1 = banks[2][0:T, 0:2 * D]
        ps_gate = banks[2][0:T, 0:R + E]
        ps_qk2 = banks[2][0:T, 0:2 * D]
        ps_v1 = banks[1][0:T, 0:D]
        ps_x2T = banks[1][:, D:D + 2 * T]
        ps_v2 = banks[7][0:T, 0:D]
        ps_slot1T = [banks[3][:, 0:HG * T], banks[4][:, 0:HG * T]]
        ps_s1 = [banks[3 + i % 2][0:T, 0:HR * T] for i in range(ROUNDS)]
        ps_z1 = banks[4][0:T, 0:D]
        ps_z1T = banks[4][:, D:D + 2 * T]
        ps_y1 = banks[3][0:T, 0:D]
        ps_slot2T = [banks[5][:, 0:HG * T], banks[6][:, 0:HG * T]]
        ps_s2 = [banks[5 + i % 2][0:T, 0:HR * T] for i in range(ROUNDS)]
        ps_pT = [banks[7 - i % 2][0:T, 0:HR * T] for i in range(ROUNDS)]
        ps_z2 = banks[6][0:T, 0:H * (DH + 1)]
        ps_z2T = banks[6][:, 256:256 + 2 * T]
        ps_y2 = banks[5][0:T, 0:D]

        weights_in = sem("weights_in")
        consts_in = sem("consts_in")
        slots_in = sem("slots_in")
        zeros_set = sem("zeros_set")
        fills_set = sem("fills_set")
        rope_set = sem("rope_set")
        x_in = [sem(f"x_in{i}") for i in range(2)]
        out_stored = sem("out_stored")
        tok_done = sem("tok_done")
        h0_set = sem("h0_set")
        stat0_set = sem("stat0_set")
        mv0_set = sem("mv0_set")
        var0_set = sem("var0_set")
        rstd0_set = sem("rstd0_set")
        xn_set = sem("xn_set")
        xnT_done = sem("xnT_done")
        xnT_copied = sem("xnT_copied")
        qk1_done = sem("qk1_done")
        v1_done = sem("v1_done")
        qk1_copied = sem("qk1_copied")
        v1_copied = sem("v1_copied")
        sq_set = sem("sq_set")
        ss_set = sem("ss_set")
        ms_set = sem("ms_set")
        rms_set = sem("rms_set")
        qkn_set = sem("qkn_set")
        own_set = sem("own_set")
        other_set = sem("other_set")
        slot1_set = sem("slot1_set")
        slot1T_done = [sem(f"slot1T_done{i}") for i in range(2)]
        slot1T_copied = [sem(f"slot1T_copied{i}") for i in range(2)]
        s1_done = [sem(f"s1_done{i}") for i in range(ROUNDS)]
        square_set = [sem(f"square_set{i}") for i in range(ROUNDS)]
        pat_set = [sem(f"pat_set{i}") for i in range(ROUNDS)]
        z1_done = sem("z1_done")
        z1_copied = sem("z1_copied")
        z1T_done = sem("z1T_done")
        z1T_copied = sem("z1T_copied")
        y1_done = sem("y1_done")
        h1_set = sem("h1_set")
        h1b_set = sem("h1b_set")
        stat1_set = sem("stat1_set")
        mv1_set = sem("mv1_set")
        var1_set = sem("var1_set")
        rstd1_set = sem("rstd1_set")
        xc_set = sem("xc_set")
        x2T_done = sem("x2T_done")
        x2T_copied = sem("x2T_copied")
        gate_done = sem("gate_done")
        nmax_set = sem("nmax_set")
        ex_set = sem("ex_set")
        rsum_set = sem("rsum_set")
        scale_set = sem("scale_set")
        top_set = sem("top_set")
        top2_set = sem("top2_set")
        rest_set = sem("rest_set")
        picked_set = sem("picked_set")
        combine_set = sem("combine_set")
        hw_set = sem("hw_set")
        catT_done = sem("catT_done")
        catT_copied = sem("catT_copied")
        qk2_done = sem("qk2_done")
        v2_done = sem("v2_done")
        slot2_set = sem("slot2_set")
        v2_copied = sem("v2_copied")
        slot2T_done = [sem(f"slot2T_done{i}") for i in range(2)]
        slot2T_copied = [sem(f"slot2T_copied{i}") for i in range(2)]
        s2_done = [sem(f"s2_done{i}") for i in range(ROUNDS)]
        smax_set = [sem(f"smax_set{i}") for i in range(ROUNDS)]
        shift_set = [sem(f"shift_set{i}") for i in range(ROUNDS)]
        prob_set = [sem(f"prob_set{i}") for i in range(ROUNDS)]
        pT_done = [sem(f"pT_done{i}") for i in range(ROUNDS)]
        pT_copied = [sem(f"pT_copied{i}") for i in range(ROUNDS)]
        z2_done = sem("z2_done")
        rden_set = sem("rden_set")
        z2_set = sem("z2_set")
        z2T_done = sem("z2T_done")
        z2T_copied = sem("z2T_copied")
        y2_done = sem("y2_done")
        out_set = sem("out_set")

        WEIGHTS = 13
        CONSTS = 5

        class Step:

            def __init__(self, eng, n, parity):
                self.eng, self.n, self.parity = eng, n, parity
                self.fixed = isinstance(n, int)

            def works(self, stage):
                return not self.fixed or 0 <= self.n - stage < TILES

            def par(self, stage):
                return (self.parity + stage) % 2

            def began(self, stage, back=0):
                return not self.fixed or self.n - stage - back >= 0

            def upto(self, stage, back=0):
                count = self.n - stage + (1 - back)
                return min(count, TILES) if self.fixed else count

            def patches(self):
                return self.n * 8 + (16 - 8 * self.parity)

        FIRST = STAGES
        STEPS = TILES + STAGES - 1

        def run(eng, step):
            for n in range(FIRST):
                step(Step(eng, n, n % 2))
            with eng.Fori(FIRST, TILES, 2) as n:
                step(Step(eng, n, 0))
                step(Step(eng, n + 1, 1))
            for n in range(TILES, STEPS):
                step(Step(eng, n, n % 2))

        block = ctx.enter_context(nc.Block())

        @block.sync
        def _(sp):
            sp.dma_start(tok_w[:, :, :], w_tok).then_inc(weights_in, 16)
            for dst, src in ((tok_b, b_tok.broadcast_to([T, D])), (ident, identity)):
                sp.dma_start(dst[:, :], src).then_inc(consts_in, 16)
            sp.dma_start(x_sb[0][:, :, :], x_tiles[0]).then_inc(x_in[0], 16)
            for dst, src in ((qkv1_w0, w_qkv1[0:P]), (qkv1_w1, w_qkv1[P:D + 1])):
                sp.dma_start(dst[:, :], src).then_inc(weights_in, 16)
            sp.dma_start(x_sb[1][:, :, :], x_tiles[1]).then_inc(x_in[1], 16)
            for dst, src in ((o1_w0, w_o1[0:P]), (o1_w1, w_o1[P:D]), (gate_w0, w_gate[0:P]),
                             (gate_w1, w_gate[P:D + 1]), (qkv2_w0, w_qkv2[0:P]),
                             (qkv2_w1, w_qkv2[P:D + 1 + E]), (lora_w, w_lora),
                             (proj_w0, w_proj[0:P]), (proj_w1, w_proj[P:D]),
                             (proj_b, b_proj.broadcast_to([T, D]))):
                sp.dma_start(dst[:, :], src).then_inc(weights_in, 16)

            x_pairs = x_tiles.rearrange("(m k) p c t -> m k p c t", k=2)
            out_pairs = out.rearrange("(m k) t d -> m k t d", k=2)

            def load(m, k):
                sp.wait_ge(tok_done, 2 * m + (k - 1))
                sp.dma_start(x_sb[k][:, :, :], x_pairs[m, k]).then_inc(x_in[k], 16)

            def store(m, k):
                sp.wait_ge(out_set, 2 * m + (k + 1))
                sp.dma_start(out_pairs[m, k], out_sb[k][:, :]).then_inc(out_stored, 16)

            load(1, 0)
            load(1, 1)
            with sp.Fori(FIRST // 2, TILES // 2) as m:
                for k in range(2):
                    load(m, k)
                    store(m - STAGES // 2, k)
            for t in range(TILES - STAGES, TILES):
                store(t // 2, t % 2)
            sp.wait_ge(out_stored, 16 * TILES)

        @block.tensor
        def _(pe):
            def transpose(dst, src):
                n = src.shape[0]
                return nc.tensor.transpose(dst, src, ident[0:n, 0:n])

            def tokens(s):
                pe.wait_ge(x_in[s.parity], s.patches())
                if s.began(0, 1):
                    pe.wait_ge(xnT_copied, s.upto(0, 1))
                for c in range(CK):
                    mm = nc.tensor.matmul(ps_tok, x_sb[s.par(0)][:, c, :], tok_w[:, c, :],
                                          start=(c == 0), stop=(c == CK - 1))
                mm.then_inc(tok_done, 1)

            def turn_xn(s):
                pe.wait_ge(xn_set, s.upto(0))
                for c in range(2):
                    mm = transpose(ps_xnT[:, c * T:(c + 1) * T], xn[:, c * P:(c + 1) * P])
                mm.then_inc(xnT_done, 1)

            def project1(s):
                pe.wait_ge(xnT_copied, s.upto(0))
                if s.began(2, 1):
                    pe.wait_ge(slot2_set, s.upto(2, 1))
                if s.began(2):
                    pe.wait_ge(hw_set, s.upto(2))
                for sem_, dst, c0, c1 in ((qk1_done, ps_qk1, 0, 2 * D), (v1_done, ps_v1, 2 * D, 3 * D)):
                    nc.tensor.matmul(dst, xnT[:, 0, :], qkv1_w0[:, c0:c1], start=True, stop=False)
                    nc.tensor.matmul(dst, xnT[0:D2 + 1, 1, :], qkv1_w1[:, c0:c1],
                                     start=False, stop=True).then_inc(sem_, 1)

            def turn_slot1(s, i):
                if i == 0:
                    pe.wait_ge(slot1_set, s.upto(1))
                    if s.began(1, 1):
                        pe.wait_ge(h1_set, s.upto(1, 1))
                else:
                    if s.began(1, 1):
                        pe.wait_ge(z1T_copied, s.upto(1, 1))
                for g in range(HG):
                    src = slot1[:, i * H + g * HPG:i * H + (g + 1) * HPG, :].rearrange("t h d -> t (h d)")
                    mm = transpose(ps_slot1T[i][:, g * T:(g + 1) * T], src)
                mm.then_inc(slot1T_done[i], 1)

            def scores1(s, i):
                pe.wait_ge(slot1T_copied[0], s.upto(1))
                pe.wait_ge(slot1T_copied[1], s.upto(1))
                if i >= 2:
                    pe.wait_ge(square_set[i - 2], s.upto(1))
                r = slice(i * SLOT, i * SLOT + DH)
                for g in range(HR):
                    mm = nc.tensor.matmul(ps_s1[i][:, g * T:(g + 1) * T], qk1T[r, 1, g, :],
                                          qk1T[r, 0, g, :], start=True, stop=True)
                mm.then_inc(s1_done[i], 1)

            def values1(s):
                pe.wait_ge(square_set[3], s.upto(1))
                for i in range(ROUNDS):
                    pe.wait_ge(pat_set[i], s.upto(1))
                    for h in range(i * HR, (i + 1) * HR):
                        mm = nc.tensor.matmul(ps_z1[:, h * DH:(h + 1) * DH], pat[:, h, :],
                                              v1[s.par(1)][:, h * DH:(h + 1) * DH],
                                              start=True, stop=True)
                mm.then_inc(z1_done, 1)

            def turn_z1(s):
                pe.wait_ge(z1_copied, s.upto(1))
                transpose(ps_z1T[:, 0:T], z1[:, 0:P])
                transpose(ps_z1T[0:D2, T:2 * T], z1[:, P:D]).then_inc(z1T_done, 1)

            def output1(s):
                pe.wait_ge(z1T_copied, s.upto(1))
                pe.wait_ge(square_set[2], s.upto(1))
                nc.tensor.matmul(ps_y1, z1T[:, 0, :], o1_w0[:, :], start=True, stop=False)
                nc.tensor.matmul(ps_y1, z1T[0:D2, 1, :], o1_w1[:, :],
                                 start=False, stop=True).then_inc(y1_done, 1)

            def turn_x2(s):
                pe.wait_ge(xc_set, s.upto(2))
                if s.began(2, 1):
                    pe.wait_ge(catT_copied, s.upto(2, 1))
                pe.wait_ge(v1_copied, s.upto(1))
                for c in range(2):
                    mm = transpose(ps_x2T[:, c * T:(c + 1) * T], xc[:, c * P:(c + 1) * P])
                mm.then_inc(x2T_done, 1)

            def gate(s):
                pe.wait_ge(x2T_copied, s.upto(2))
                if s.began(2, 1):
                    pe.wait_ge(slot2_set, s.upto(2, 1))
                pe.wait_ge(qk1_copied, s.upto(1))
                nc.tensor.matmul(ps_gate, x2T[:, 0, :], gate_w0[:, :], start=True, stop=False)
                nc.tensor.matmul(ps_gate, x2T[0:D2 + 1, 1, :], gate_w1[:, :],
                                 start=False, stop=True).then_inc(gate_done, 1)

            def turn_cat(s):
                pe.wait_ge(combine_set, s.upto(2))
                pe.wait_ge(hw_set, s.upto(2))
                pe.wait_ge(v1_copied, s.upto(0))
                transpose(ps_x2T[:, 0:T], xc[:, P:2 * P])
                transpose(ps_x2T[:, T:2 * T], hw[:, :, :].rearrange("t e r -> t (e r)"))\
                    .then_inc(catT_done, 1)

            def project2(s):
                pe.wait_ge(catT_copied, s.upto(2))
                pe.wait_ge(qk1_copied, s.upto(0))
                if s.began(3):
                    pe.wait_ge(pT_copied[2], s.upto(3))
                for sem_, dst, c0, c1 in ((qk2_done, ps_qk2, 0, 2 * D), (v2_done, ps_v2, 2 * D, 3 * D)):
                    nc.tensor.matmul(dst, x2T[:, 0, :], qkv2_w0[:, c0:c1], start=True, stop=False)
                    nc.tensor.matmul(dst, catT[0:D2 + 1 + E, 0, :], qkv2_w1[:, c0:c1],
                                     start=False, stop=False)
                    nc.tensor.matmul(dst, catT[:, 1, :], lora_w[:, c0:c1],
                                     start=False, stop=True).then_inc(sem_, 1)

            def turn_slot2(s, i):
                if i == 0:
                    pe.wait_ge(slot2_set, s.upto(3))
                    if s.began(3, 1):
                        pe.wait_ge(out_set, s.upto(3, 1))
                else:
                    if s.began(3, 1):
                        pe.wait_ge(z2T_copied, s.upto(3, 1))
                for g in range(HG):
                    src = slot2[:, i * H + g * HPG:i * H + (g + 1) * HPG, :].rearrange("t h d -> t (h d)")
                    mm = transpose(ps_slot2T[i][:, g * T:(g + 1) * T], src)
                mm.then_inc(slot2T_done[i], 1)

            def scores2(s, i):
                pe.wait_ge(slot2T_copied[0], s.upto(3))
                pe.wait_ge(slot2T_copied[1], s.upto(3))
                if i >= 2:
                    pe.wait_ge(shift_set[i - 2], s.upto(3))
                r = slice(i * SLOT, i * SLOT + KX)
                for g in range(HR):
                    mm = nc.tensor.matmul(ps_s2[i][:, g * T:(g + 1) * T], qk2T[r, 0, g, :],
                                          qk2T[r, 1, g, :], start=True, stop=True)
                mm.then_inc(s2_done[i], 1)

            def turn_prob(s, i):
                pe.wait_ge(prob_set[i], s.upto(3))
                if i == 0:
                    pe.wait_ge(v2_copied, s.upto(3))
                elif i == 1:
                    pe.wait_ge(shift_set[3], s.upto(3))
                else:
                    pe.wait_ge(pT_copied[i - 2], s.upto(3))
                for g in range(HR):
                    mm = transpose(ps_pT[i][:, g * T:(g + 1) * T], prob[:, i * HR + g, :])
                mm.then_inc(pT_done[i], 1)

            def values2(s):
                pe.wait_ge(pT_copied[3], s.upto(3))
                for i in range(ROUNDS):
                    pe.wait_ge(pT_copied[i], s.upto(3))
                    for h in range(i * HR, (i + 1) * HR):
                        mm = nc.tensor.matmul(ps_z2[:, h * (DH + 1):(h + 1) * (DH + 1)],
                                              probT[:, h, :], v2[s.par(3)][:, h, :],
                                              start=True, stop=True)
                mm.then_inc(z2_done, 1)

            def turn_z2(s):
                pe.wait_ge(z2_set, s.upto(3))
                z = z2[:, :, :].rearrange("t h d -> t (h d)")
                transpose(ps_z2T[:, 0:T], z[:, 0:P])
                transpose(ps_z2T[0:D2, T:2 * T], z[:, P:D]).then_inc(z2T_done, 1)

            def output2(s):
                pe.wait_ge(z2T_copied, s.upto(3))
                pe.wait_ge(shift_set[2], s.upto(3))
                nc.tensor.matmul(ps_y2, z2T[:, 0, :], proj_w0[:, :], start=True, stop=False)
                nc.tensor.matmul(ps_y2, z2T[0:D2, 1, :], proj_w1[:, :],
                                 start=False, stop=True).then_inc(y2_done, 1)

            def step(s):
                s0, s1, s2, s3 = (s.works(k) for k in range(STAGES))
                if s3: turn_slot2(s, 0); turn_slot2(s, 1)
                if s0: tokens(s)
                if s1: turn_slot1(s, 0); turn_slot1(s, 1)
                if s3: scores2(s, 0); scores2(s, 1)
                if s2: turn_x2(s)
                if s1: scores1(s, 0)
                if s0: turn_xn(s)
                if s1: scores1(s, 1)
                if s3: scores2(s, 2)
                if s2: gate(s)
                if s3: scores2(s, 3); turn_prob(s, 0)
                if s1: scores1(s, 2)
                if s3: turn_prob(s, 1)
                if s0: project1(s)
                if s1: scores1(s, 3)
                if s3: turn_prob(s, 2); turn_prob(s, 3)
                if s2: turn_cat(s)
                if s1: values1(s)
                if s3: values2(s)
                if s1: turn_z1(s)
                if s2: project2(s)
                if s3: turn_z2(s)
                if s1: output1(s)
                if s3: output2(s)

            pe.wait_ge(weights_in, 16 * WEIGHTS)
            pe.wait_ge(consts_in, 16 * CONSTS)
            run(pe, step)

        @block.scalar
        def _(act):
            copy = nc.scalar.copy

            def copy_xnT(s):
                act.wait_ge(xnT_done, s.upto(0))
                copy(xnT[:, :, :], ps_xnT.rearrange("p (c t) -> p c t", c=2)).then_inc(xnT_copied, 1)

            def copy_qk1(s):
                act.wait_ge(qk1_done, s.upto(0))
                if s.began(0, 2):
                    act.wait_ge(qkn_set, s.upto(0, 2))
                copy(qk1[s.par(0)][:, :, :].rearrange("t h d -> t (h d)"), ps_qk1).then_inc(qk1_copied, 1)
                act.wait_ge(v1_done, s.upto(0))
                if s.began(0, 2):
                    act.wait_ge(z1_done, s.upto(0, 2))
                copy(v1[s.par(0)][:, :], ps_v1).then_inc(v1_copied, 1)

            def copy_slot1T(s, i):
                act.wait_ge(slot1T_done[i], s.upto(1))
                copy(qk1T[:, i, :, :], ps_slot1T[i].rearrange("p (g t) -> p g t", g=HG))\
                    .then_inc(slot1T_copied[i], 1)

            def squares(s, g):
                act.wait_ge(s1_done[g], s.upto(1))
                if g == 0:
                    if s.began(1, 1):
                        act.wait_ge(z1_done, s.upto(1, 1))
                nc.scalar.activation(pat[:, g * HR:(g + 1) * HR, :],
                                     ps_s1[g].rearrange("t (h k) -> t h k", h=HR),
                                     ACT.Square, scale=1.0 / DH).then_inc(square_set[g], 1)

            def copy_z1(s):
                act.wait_ge(z1_done, s.upto(1))
                copy(z1[:, :], ps_z1).then_inc(z1_copied, 1)

            def copy_z1T(s):
                act.wait_ge(z1T_done, s.upto(1))
                copy(z1T[:, 0, :], ps_z1T[:, 0:T])
                copy(z1T[0:D2, 1, :], ps_z1T[0:D2, T:2 * T]).then_inc(z1T_copied, 1)

            def copy_x2T(s):
                act.wait_ge(x2T_done, s.upto(2))
                if s.began(2, 1):
                    act.wait_ge(qk2_done, s.upto(2, 1))
                if s.began(2, 1):
                    act.wait_ge(v2_done, s.upto(2, 1))
                copy(x2T[:, :, :], ps_x2T.rearrange("p (c t) -> p c t", c=2)).then_inc(x2T_copied, 1)

            def router_exp(s):
                act.wait_ge(nmax_set, s.upto(2))
                if s.began(2, 1):
                    act.wait_ge(picked_set, s.upto(2, 1))
                nc.scalar.activation(ex[:, 0:E], ps_gate[:, R:R + E], ACT.Exp, bias=nmax[:, 0:1],
                                     accum_out=exsum[:, 0:1]).then_inc(ex_set, 1)

            def copy_catT(s):
                act.wait_ge(catT_done, s.upto(2))
                copy(catT[:, :, :], ps_x2T.rearrange("p (c t) -> p c t", c=2)).then_inc(catT_copied, 1)

            def copy_qkv2(s):
                act.wait_ge(qk2_done, s.upto(2))
                if s.began(3):
                    act.wait_ge(slot2T_done[1], s.upto(3))
                copy(slot2[:, :, 0:DH], ps_qk2.rearrange("t (h d) -> t h d", d=DH)).then_inc(slot2_set, 1)
                act.wait_ge(v2_done, s.upto(2))
                if s.began(2, 2):
                    act.wait_ge(z2_done, s.upto(2, 2))
                copy(v2[s.par(2)][:, :, 0:DH], ps_v2.rearrange("t (h d) -> t h d", d=DH))\
                    .then_inc(v2_copied, 1)

            def copy_slot2T(s, i):
                act.wait_ge(slot2T_done[i], s.upto(3))
                copy(qk2T[:, i, :, :], ps_slot2T[i].rearrange("p (g t) -> p g t", g=HG))\
                    .then_inc(slot2T_copied[i], 1)

            def probs(s, g):
                act.wait_ge(shift_set[g], s.upto(3))
                heads = prob[:, g * HR:(g + 1) * HR, :]
                nc.scalar.activation(heads, heads, ACT.Exp, scale=SM_SCALE).then_inc(prob_set[g], 1)

            def copy_probT(s, g):
                act.wait_ge(pT_done[g], s.upto(3))
                if g == 0:
                    if s.began(3, 1):
                        act.wait_ge(z2_done, s.upto(3, 1))
                copy(probT[:, g * HR:(g + 1) * HR, :],
                     ps_pT[g].rearrange("t (h k) -> t h k", h=HR)).then_inc(pT_copied[g], 1)

            def copy_z2T(s):
                act.wait_ge(z2T_done, s.upto(3))
                copy(z2T[:, 0, :], ps_z2T[:, 0:T])
                copy(z2T[0:D2, 1, :], ps_z2T[0:D2, T:2 * T]).then_inc(z2T_copied, 1)

            def step(s):
                s0, s1, s2, s3 = (s.works(k) for k in range(STAGES))
                if s3: copy_slot2T(s, 0); copy_slot2T(s, 1)
                if s1: copy_slot1T(s, 0); copy_slot1T(s, 1)
                if s2: copy_x2T(s)
                if s1: squares(s, 0)
                if s0: copy_xnT(s)
                if s1: squares(s, 1)
                if s3: probs(s, 0); probs(s, 1)
                if s2: router_exp(s)
                if s3: probs(s, 2)
                if s1: squares(s, 2)
                if s3: copy_probT(s, 0); probs(s, 3)
                if s0: copy_qk1(s)
                if s1: squares(s, 3)
                if s3: copy_probT(s, 2)
                if s2: copy_catT(s)
                if s1: copy_z1(s)
                if s1: copy_z1T(s)
                if s2: copy_qkv2(s)
                if s3: copy_z2T(s)

            act.dma_start(g_sb[:, :], g_rows.broadcast_to([T, 2 * DH])).then_inc(consts_in, 16)
            act.dma_start(rope_sb[:, :], rope_rows).then_inc(consts_in, 16)
            act.dma_start(keep[:, :], causal_keep).then_inc(consts_in, 16)
            for i in range(2):
                act.dma_start(slot2[:, i * H:(i + 1) * H, DH:SLOT], image_rows[:, i]).then_inc(slots_in, 16)
            act.wait_ge(slots_in, 16 * 2)
            run(act, step)

        @block.vector
        def _(dve):
            def embed(s):
                dve.wait_ge(tok_done, s.upto(0))
                if s.began(0, 2):
                    dve.wait_ge(h1_set, s.upto(0, 2))
                if s.began(0, 1):
                    dve.wait_ge(xn_set, s.upto(0, 1))
                nc.vector.tensor_tensor(h0[s.par(0)][:, :], ps_tok, tok_b[:, :], ALU.add).then_inc(h0_set, 1)

            def stats(s, stage, src, src_sem, stat, stat_sem):
                dve.wait_ge(src_sem, s.upto(stage))
                nc.vector.bn_stats(stat[:, :], src[:, :]).then_inc(stat_sem, 1)

            def moments(mv, stat, mv_sem):
                nc.vector.bn_aggr(mv[:, :], stat[:, :]).then_inc(mv_sem, 1)

            def variance(s, stage, mv, mv_sem, var, var_sem):
                dve.wait_ge(mv_sem, s.upto(stage))
                nc.vector.tensor_scalar(var[:, :], mv[:, 1:2], LN_EPS, None, ALU.add).then_inc(var_sem, 1)

            def normalize0(s):
                dve.wait_ge(rstd0_set, s.upto(0))
                if s.began(0, 1):
                    dve.wait_ge(xnT_done, s.upto(0, 1))
                nc.vector.tensor_scalar(xn[:, 0:D], h0[s.par(0)][:, :], mv0[:, 0:1], rstd0[:, 0:1],
                                        ALU.subtract, ALU.mult).then_inc(xn_set, 1)

            def normalize1(s):
                dve.wait_ge(rstd1_set, s.upto(2))
                if s.began(2, 1):
                    dve.wait_ge(catT_done, s.upto(2, 1))
                nc.vector.tensor_scalar(xc[:, 0:D], h1[s.par(2)][:, :], mv1[:, 0:1], rstd1[:, 0:1],
                                        ALU.subtract, ALU.mult).then_inc(xc_set, 1)

            def head_sums(s):
                dve.wait_ge(sq_set, s.upto(1))
                nc.vector.tensor_reduce(ss[:, :], sq[:, :, :], AX.X, ALU.add).then_inc(ss_set, 1)
                dve.wait_ge(ss_set, s.upto(1))
                nc.vector.tensor_scalar(ms[:, :], ss[:, :], 1.0 / DH, RMS_EPS, ALU.mult, ALU.add)\
                    .then_inc(ms_set, 1)

            def head_norm(s):
                dve.wait_ge(rms_set, s.upto(1))
                if s.began(1, 1):
                    dve.wait_ge(own_set, s.upto(1, 1))
                nc.vector.tensor_tensor(qkn[:, :, :], qk1[s.par(1)][:, :, :],
                                        rms[:, :].unsqueeze(2).broadcast_to([T, 2 * H, DH]),
                                        ALU.mult).then_inc(qkn_set, 1)

            def rotate(s):
                dve.wait_ge(qkn_set, s.upto(1))
                if s.began(1, 1):
                    dve.wait_ge(slot1_set, s.upto(1, 1))
                for i in range(2):
                    dst = slice(i * HALF, (i + 1) * HALF)
                    src = slice((1 - i) * HALF, (2 - i) * HALF)
                    table = rope[:, DH + i * HALF:DH + (i + 1) * HALF].unsqueeze(1)
                    op = nc.vector.tensor_tensor(other[:, :, dst], qkn[:, :, src],
                                                 table.broadcast_to([T, 2 * H, HALF]), ALU.mult)
                op.then_inc(other_set, 1)
                dve.wait_ge(other_set, s.upto(1))
                dve.wait_ge(own_set, s.upto(1))
                if s.began(1, 1):
                    dve.wait_ge(slot1T_done[1], s.upto(1, 1))
                nc.vector.tensor_tensor(slot1[:, :, 0:DH], own[:, :, :], other[:, :, :], ALU.add)\
                    .then_inc(slot1_set, 1)

            def residual1(s):
                dve.wait_ge(y1_done, s.upto(1))
                if s.began(1, 2):
                    dve.wait_ge(xc_set, s.upto(1, 2))
                if s.began(1, 2):
                    dve.wait_ge(h1b_set, s.upto(1, 2))
                nc.vector.tensor_tensor(h1[s.par(1)][:, :], ps_y1, h0[s.par(1)][:, :], ALU.add)\
                    .then_inc(h1_set, 1)

            def router_max(s):
                dve.wait_ge(gate_done, s.upto(2))
                nc.vector.tensor_reduce(nmax[:, :], ps_gate[:, R:R + E], AX.X, ALU.max, negate=True)\
                    .then_inc(nmax_set, 1)

            def route(s):
                dve.wait_ge(ex_set, s.upto(2))
                nc.vector.reciprocal(rsum[:, :], exsum[:, :]).then_inc(rsum_set, 1)
                nc.vector.max(top[:, :], ex[:, 0:E]).then_inc(top_set, 1)
                dve.wait_ge(top_set, s.upto(2))
                nc.vector.tensor_copy(top2[:, 0:2], top[:, 0:2]).then_inc(top2_set, 1)
                dve.wait_ge(rsum_set, s.upto(2))
                dve.wait_ge(top2_set, s.upto(2))
                nc.vector.tensor_scalar(lora_scale[:, :], rsum[:, :], LORA_SCALE, None, ALU.mult)\
                    .then_inc(scale_set, 1)
                nc.vector.match_replace(rest[:, :], top2[:, :], ex[:, :], 0.0).then_inc(rest_set, 1)
                dve.wait_ge(rest_set, s.upto(2))
                nc.vector.tensor_tensor(picked[:, :], ex[:, 0:E], rest[:, 0:E], ALU.subtract)\
                    .then_inc(picked_set, 1)
                dve.wait_ge(picked_set, s.upto(2))
                dve.wait_ge(scale_set, s.upto(2))
                dve.wait_ge(x2T_done, s.upto(2))
                nc.vector.tensor_scalar(xc[:, D + 1:D + 1 + E], picked[:, :], lora_scale[:, 0:1], None,
                                        ALU.mult).then_inc(combine_set, 1)
                dve.wait_ge(combine_set, s.upto(2))
                nc.vector.tensor_tensor(
                    hw[:, :, :], ps_gate[:, 0:R].rearrange("t (e r) -> t e r", e=E),
                    xc[:, D + 1:D + 1 + E].unsqueeze(2).broadcast_to([T, E, RANK]),
                    ALU.mult).then_inc(hw_set, 1)

            def shift(s, g):
                dve.wait_ge(s2_done[g], s.upto(3))
                heads = slice(g * HR, (g + 1) * HR)
                scores = ps_s2[g].rearrange("t (h k) -> t h k", h=HR)
                nc.vector.tensor_reduce(smax[:, heads], scores, AX.X, ALU.max).then_inc(smax_set[g], 1)
                dve.wait_ge(smax_set[g], s.upto(3))
                if s.began(3, 1):
                    dve.wait_ge(pT_done[g], s.upto(3, 1))
                nc.vector.tensor_tensor(prob[:, heads, :], scores,
                                        smax[:, heads].unsqueeze(2).broadcast_to([T, HR, T]),
                                        ALU.subtract).then_inc(shift_set[g], 1)

            def copy_probT(s, g):
                dve.wait_ge(pT_done[g], s.upto(3))
                nc.vector.tensor_copy(probT[:, g * HR:(g + 1) * HR, :],
                                      ps_pT[g].rearrange("t (h k) -> t h k", h=HR))\
                    .then_inc(pT_copied[g], 1)

            def divide(s):
                dve.wait_ge(z2_done, s.upto(3))
                z = ps_z2.rearrange("t (h d) -> t h d", d=DH + 1)
                nc.vector.reciprocal(rden[:, :], z[:, :, DH]).then_inc(rden_set, 1)
                dve.wait_ge(rden_set, s.upto(3))
                nc.vector.tensor_tensor(z2[:, :, :], z[:, :, 0:DH],
                                        rden[:, :].unsqueeze(2).broadcast_to([T, H, DH]),
                                        ALU.mult).then_inc(z2_set, 1)

            def residual2(s):
                dve.wait_ge(y2_done, s.upto(3))
                dve.wait_ge(h1b_set, s.upto(3))
                if s.began(3, 1):
                    dve.wait_ge(out_stored, s.upto(3, 1) * 16)
                nc.vector.tensor_tensor(out_sb[s.par(3)][:, :], ps_y2, h1b[s.par(3)][:, :], ALU.add)\
                    .then_inc(out_set, 1)

            def step(s):
                s0, s1, s2, s3 = (s.works(k) for k in range(STAGES))
                if s2:
                    stats(s, 2, h1[s.par(2)], h1_set, stat1, stat1_set)
                    dve.wait_ge(stat1_set, s.upto(2))
                if s0: embed(s)
                if s2: moments(mv1, stat1, mv1_set)
                if s0:
                    stats(s, 0, h0[s.par(0)], h0_set, stat0, stat0_set)
                    dve.wait_ge(stat0_set, s.upto(0))
                if s2: variance(s, 2, mv1, mv1_set, var1, var1_set)
                if s0:
                    moments(mv0, stat0, mv0_set)
                    variance(s, 0, mv0, mv0_set, var0, var0_set)
                if s2: normalize1(s)
                if s3: shift(s, 0)
                if s0: normalize0(s)
                if s3: shift(s, 1)
                if s3: shift(s, 2)
                if s2: router_max(s)
                if s3: shift(s, 3)
                if s2: route(s)
                if s3: copy_probT(s, 1); copy_probT(s, 3)
                if s3: divide(s)
                if s1: residual1(s)
                if s3: residual2(s)
                next_ = Step(s.eng, s.n + 1, 1 - s.parity)
                if not s.fixed or next_.works(1):
                    head_sums(next_); head_norm(next_); rotate(next_)

            dve.wait_ge(zeros_set, 4)
            nc.vector.memset(xn[:, D:D + 1], 1.0)
            nc.vector.memset(xc[:, D:D + 1], 1.0)
            nc.vector.memset(ex[:, E:2 * E], -1.0)
            nc.vector.memset(top2[:, :], -1.0)
            for i in range(2):
                nc.vector.memset(v2[i][:, :, DH:DH + 1], 1.0)
            dve.wait_ge(consts_in, 16 * CONSTS)
            nc.vector.tensor_tensor(rope[:, :], rope_sb[:, :], g_sb[:, :], ALU.mult).then_inc(rope_set, 1)
            dve.wait_ge(rope_set, 1)
            dve.wait_ge(weights_in, 16 * WEIGHTS)
            run(dve, step)

        @block.gpsimd
        def _(pool):
            def rstd0_(s):
                pool.wait_ge(var0_set, s.upto(0))
                if s.began(0, 1):
                    pool.wait_ge(xn_set, s.upto(0, 1))
                nc.gpsimd.tensor_tensor(rstd0[:, :], var0[:, :], minus_half[:, 0:1], ALU.pow)\
                    .then_inc(rstd0_set, 1)

            def rstd1_(s):
                pool.wait_ge(var1_set, s.upto(2))
                if s.began(2, 1):
                    pool.wait_ge(xc_set, s.upto(2, 1))
                nc.gpsimd.tensor_tensor(rstd1[:, :], var1[:, :], minus_half[:, 0:1], ALU.pow)\
                    .then_inc(rstd1_set, 1)

            def square_qk(s):
                pool.wait_ge(qk1_copied, s.upto(1))
                if s.began(1, 1):
                    pool.wait_ge(ss_set, s.upto(1, 1))
                q = qk1[s.par(1)][:, :, :]
                nc.gpsimd.tensor_tensor(sq[:, :, :], q, q, ALU.mult).then_inc(sq_set, 1)

            def rms_(s):
                pool.wait_ge(ms_set, s.upto(1))
                if s.began(1, 1):
                    pool.wait_ge(qkn_set, s.upto(1, 1))
                nc.gpsimd.tensor_tensor(rms[:, :], ms[:, :], minus_half[:, :], ALU.pow)\
                    .then_inc(rms_set, 1)

            def own_half(s):
                pool.wait_ge(qkn_set, s.upto(1))
                if s.began(1, 1):
                    pool.wait_ge(slot1_set, s.upto(1, 1))
                nc.gpsimd.tensor_tensor(own[:, :, :], qkn[:, :, :],
                                        rope[:, 0:DH].unsqueeze(1).broadcast_to([T, 2 * H, DH]),
                                        ALU.mult).then_inc(own_set, 1)

            def mask(s, g):
                pool.wait_ge(square_set[g], s.upto(1))
                heads = pat[:, g * HR:(g + 1) * HR, :]
                nc.gpsimd.tensor_tensor(heads, heads, keep[:, :].unsqueeze(1).broadcast_to([T, HR, T]),
                                        ALU.mult).then_inc(pat_set[g], 1)

            def add_bias(s):
                pool.wait_ge(h1_set, s.upto(1))
                if s.began(1, 2):
                    pool.wait_ge(out_set, s.upto(1, 2))
                nc.gpsimd.tensor_tensor(h1b[s.par(1)][:, :], h1[s.par(1)][:, :], proj_b[:, :], ALU.add)\
                    .then_inc(h1b_set, 1)

            def step(s):
                s0, s1, s2, s3 = (s.works(k) for k in range(STAGES))
                if s2: rstd1_(s)
                if s0: rstd0_(s)
                if s1: mask(s, 0); mask(s, 1); mask(s, 2); mask(s, 3)
                if s1: add_bias(s)
                next_ = Step(s.eng, s.n + 1, 1 - s.parity)
                if not s.fixed or next_.works(1):
                    square_qk(next_); rms_(next_); own_half(next_)

            for z in (xn, xc):
                nc.gpsimd.memset(z[:, :], 0.0).then_inc(zeros_set, 1)
            nc.gpsimd.memset(slot1[:, :, :], 0.0).then_inc(zeros_set, 1)
            nc.gpsimd.memset(minus_half[:, :], -0.5).then_inc(zeros_set, 1)
            pool.wait_ge(zeros_set, 4)
            pool.wait_ge(rope_set, 1)
            pool.wait_ge(weights_in, 16 * WEIGHTS)
            run(pool, step)


def kernel(**inputs):
    import numpy as np
    import concourse.bacc as bacc
    from concourse.bass_utils import run_bass_kernel_spmd

    IMG, C, SIDE, PATCH, PER_TILE = 64, 3, 96, 16, 3
    H, DH, D, BASE = 12, 16, 192, 512.0
    N = SIDE // PATCH
    S = N * N
    TILES = -(-IMG // PER_TILE)
    T = PER_TILE * S

    x = np.asarray(inputs["x"])
    starts = [min(PER_TILE * t, IMG - PER_TILE) for t in range(TILES)]
    xt = x.reshape(IMG, C, N, PATCH, N, PATCH).transpose(1, 3, 5, 0, 2, 4).reshape(-1, 128, IMG, S)
    x_tiles = np.stack([xt[:, :, a:a + PER_TILE] for a in starts])
    x_tiles = x_tiles.transpose(0, 2, 1, 3, 4).reshape(TILES, 128, -1, T)

    g = {n: np.asarray(a) for n, a in inputs.items() if n != "x"}

    def strips(a):
        return a.reshape(4, 3, DH, -1).transpose(1, 0, 2, 3).reshape(a.shape)

    for c in "qk":
        for n in ("L0_attn_W", "L0_attn_b"):
            g[n + c] = strips(g[n + c])

    def strips_qkv(a):
        return np.concatenate([strips(a[:D]), strips(a[D:2 * D]), a[2 * D:]], 0)

    g["L0_ffn_Wqkv"] = strips_qkv(g["L0_ffn_Wqkv"])
    g["L0_ffn_bqkv"] = strips_qkv(g["L0_ffn_bqkv"])
    g["L0_ffn_bb"] = np.stack([strips_qkv(a) for a in g["L0_ffn_bb"]])
    g["L0_ffn_Bm"] = np.stack([strips_qkv(a) for a in g["L0_ffn_Bm"]])
    row = lambda n: g[n].reshape(1, -1)
    w_tok = g["L0_tok_W"].T.reshape(-1, 128, D).transpose(1, 0, 2)
    w_qkv1 = np.concatenate([np.concatenate([g["L0_attn_W" + c].T for c in "qkv"], 1),
                             np.concatenate([row("L0_attn_b" + c) for c in "qkv"], 1)], 0)
    a = g["L0_ffn_A"].reshape(-1, D)
    w_gate = np.concatenate([np.concatenate([a.T, g["L0_ffn_Wg"].T], 1),
                             np.concatenate([row("L0_ffn_ba"), row("L0_ffn_bg")], 1)], 0)
    w_qkv2 = np.concatenate([g["L0_ffn_Wqkv"].T, row("L0_ffn_bqkv"), g["L0_ffn_bb"]], 0)
    w_lora = g["L0_ffn_Bm"].transpose(0, 2, 1).reshape(-1, 3 * D)
    gain = g["L0_attn_g"]
    g_rows = np.concatenate([gain, gain[DH // 2:], gain[:DH // 2]]).reshape(1, -1)

    inv = (1.0 / BASE ** (np.arange(0, DH, 2, dtype=np.float32) / DH)).astype(np.float32)
    at = np.arange(T)
    freqs = np.outer((at % S).astype(np.float32), inv).astype(np.float32)
    cos, sin = np.cos(freqs), np.sin(freqs)
    rope_rows = np.concatenate([cos, cos, sin, -sin], 1).astype(np.float32)
    same = (at[:, None] // S) == (at[None, :] // S)
    causal_keep = (same & (at[:, None] <= at[None, :])).astype(np.float32)
    image = (at[:, None] // S == np.arange(PER_TILE)[None, :]).astype(np.float32)
    image_rows = np.zeros((T, 2, H, 32 - DH), np.float32)
    image_rows[:, 0, :, 0:PER_TILE] = image[:, None, :]
    image_rows[:, 1, :, 0:PER_TILE] = (1.0 - image[:, None, :]) * np.float32(-1e30)
    identity = np.eye(128, dtype=np.float32)

    nc = bacc.Bacc("TRN2", target_bir_lowering=False, num_devices=1)
    arrays = dict(x_tiles=x_tiles, w_tok=w_tok, b_tok=row("L0_tok_b"), w_qkv1=w_qkv1,
                  w_o1=g["L0_attn_Wo"].T, g_rows=g_rows, rope_rows=rope_rows,
                  causal_keep=causal_keep, w_gate=w_gate, w_qkv2=w_qkv2, w_lora=w_lora,
                  w_proj=g["L0_ffn_Wproj"].T, b_proj=row("L0_ffn_bproj"),
                  image_rows=image_rows, identity=identity)
    arrays = {n: np.ascontiguousarray(v) for n, v in arrays.items()}
    args = {n: nc.dram_tensor("in_" + n, v.shape, mybir.dt.from_np(v.dtype), kind="ExternalInput").ap()
            for n, v in arrays.items()}
    args["out"] = nc.dram_tensor("out_h", (TILES, T, D), mybir.dt.float32, kind="ExternalOutput").ap()
    vit_tower(nc, **args)
    r = run_bass_kernel_spmd(nc, [{"in_" + n: v for n, v in arrays.items()}], core_ids=[0])
    h = r.results[0]["out_h"].reshape(TILES, PER_TILE, S, D)
    own = PER_TILE * (TILES - 1) - starts[-1]
    return np.concatenate([h[:-1].reshape(-1, S, D), h[-1, own:]], 0)
```

```python
import concourse.bass as bass
from concourse import mybir
from contextlib import ExitStack


def vit_tower(nc, x_tiles, w_tok, b_tok, w_qkv1, w_o1, g_rows, rope_rows, causal_keep,
              w_gate, w_qkv2, w_lora, w_proj, b_proj, image_rows, identity, out):
    fp32 = mybir.dt.float32
    fp32r = mybir.dt.float32r
    ALU = mybir.AluOpType
    ACT = mybir.ActivationFunctionType
    AX = mybir.AxisListType

    TILES, P, CK, T = x_tiles.shape
    D = w_tok.shape[2]
    H = 12
    DH = D // H
    HALF = DH // 2
    D2 = D - P
    SLOT = 64
    STRIPS = P // SLOT
    GROUPS = H // STRIPS
    HR = 3
    ROUNDS = H // HR
    VSLOT = 32
    VSTRIPS = P // VSLOT
    VGROUPS = H // VSTRIPS
    E = 8
    R = w_lora.shape[0]
    RANK = R // E
    SPLIT = 3 * DH
    KX = SPLIT + 3
    LN_EPS = 1e-5
    RMS_EPS = 1e-6
    LORA_SCALE = 2.0
    SM_SCALE = DH ** -0.5
    STAGES = 5

    with ExitStack() as ctx:
        def sb(name, shape, dtype=fp32):
            return ctx.enter_context(nc.sbuf_tensor(name, shape, dtype))

        def bank(name):
            return ctx.enter_context(nc.psum_tensor(name, [P, 512], fp32))

        def sem(name):
            return ctx.enter_context(nc.semaphore(name))

        tok_w = sb("tok_w", [P, CK, D])
        tok_b = sb("tok_b", [T, D])
        qkv1_w0 = sb("qkv1_w0", [P, 3 * D])
        qkv1_w1 = sb("qkv1_w1", [D2 + 1, 3 * D])
        o1_w = sb("o1_w", [P, VGROUPS, D])
        gate_w0 = sb("gate_w0", [P, R + E])
        gate_w1 = sb("gate_w1", [D2 + 1, R + E])
        qkv2_w0 = sb("qkv2_w0", [P, 3 * D])
        qkv2_w1 = sb("qkv2_w1", [D2 + 1 + E, 3 * D])
        lora_w = sb("lora_w", [R, 3 * D])
        proj_w0 = sb("proj_w0", [P, D])
        proj_w1 = sb("proj_w1", [D2, D])
        proj_b = sb("proj_b", [T, D])
        ident = sb("ident", [P, P])
        keep = sb("keep", [T, T])
        g_sb = sb("g_sb", [T, 2 * DH])
        rope_sb = sb("rope_sb", [T, 2 * DH])
        rope = sb("rope", [T, 2 * DH])
        minus_half = sb("minus_half", [T, 2 * H])

        x_sb = [sb(f"x_sb{i}", [P, CK, T]) for i in range(2)]
        out_sb = [sb(f"out_sb{i}", [T, D]) for i in range(2)]
        h0 = [sb(f"h0_{i}", [T, D]) for i in range(2)]
        qk1 = [sb(f"qk1_{i}", [T, 2 * H, DH]) for i in range(2)]
        v1 = [sb(f"v1_{i}", [T, H, VSLOT]) for i in range(2)]
        h1 = [sb(f"h1_{i}", [T, D]) for i in range(2)]
        h1b = [sb(f"h1b_{i}", [T, D]) for i in range(2)]
        v2 = [sb(f"v2_{i}", [T, H, VSLOT]) for i in range(2)]

        stat0 = sb("stat0", [T, 6])
        mv0 = sb("mv0", [T, 2])
        var0 = sb("var0", [T, 1])
        rstd0 = sb("rstd0", [T, 1])
        xn = sb("xn", [T, 2 * P])
        xnT = sb("xnT", [P, 2, T])
        sq = sb("sq", [T, 2 * H, DH])
        ss = sb("ss", [T, 2 * H])
        ms = sb("ms", [T, 2 * H])
        rms = sb("rms", [T, 2 * H])
        qkn = sb("qkn", [T, 2 * H, DH])
        own = sb("own", [T, 2 * H, DH])
        other = sb("other", [T, 2 * H, DH])
        qkr = sb("qkr", [T, 2 * H, DH])
        slot1 = sb("slot1", [T, 2 * H, SLOT], fp32r)
        qk1T = sb("qk1T", [P, 2, GROUPS, T], fp32r)
        pat = sb("pat", [T, H, T])
        z1T = sb("z1T", [P, VGROUPS, T])
        stat1 = sb("stat1", [T, 6])
        mv1 = sb("mv1", [T, 2])
        var1 = sb("var1", [T, 1])
        rstd1 = sb("rstd1", [T, 1])
        xc = sb("xc", [T, 2 * P])
        x2T = sb("x2T", [P, 2, T])
        nmax = sb("nmax", [T, 1])
        ex = sb("ex", [T, 2 * E])
        exsum = sb("exsum", [T, 1])
        rsum = sb("rsum", [T, 1])
        lora_scale = sb("lora_scale", [T, 1])
        top = sb("top", [T, E])
        top2 = sb("top2", [T, E])
        rest = sb("rest", [T, 2 * E])
        picked = sb("picked", [T, E])
        hw = sb("hw", [T, E, RANK])
        catT = sb("catT", [P, 2, T])
        slot2 = sb("slot2", [T, 2 * H, SLOT], fp32r)
        qk2T = sb("qk2T", [P, 2, GROUPS, T], fp32r)
        smax = sb("smax", [T, H])
        prob = sb("prob", [T, H, T])
        probT = sb("probT", [T, H, T])
        zsT = sb("zsT", [P, VGROUPS, T])
        rden = sb("rden", [T, H])
        z2 = sb("z2", [T, H, DH])
        z2T = sb("z2T", [P, 2, T])

        banks = [bank(f"bank{i}") for i in range(8)]

        ps_zs = banks[0][0:T, 0:H * VSLOT]
        ps_z2T = banks[0][:, 0:2 * T]
        ps_y2 = banks[0][0:T, 0:D]
        ps_tok = banks[0][0:T, 0:D]
        ps_xnT = banks[0][:, D:D + 2 * T]
        ps_qk1 = banks[2][0:T, 0:2 * D]
        ps_gate = banks[2][0:T, 0:R + E]
        ps_qk2 = banks[2][0:T, 0:2 * D]
        ps_v1 = banks[1][0:T, 0:D]
        ps_x2T = banks[1][:, D:D + 2 * T]
        ps_v2 = banks[7][0:T, 0:D]
        ps_slot1T = [banks[3 + i % 2][:, 0:HR * T] for i in range(4)]
        ps_s1 = [banks[3 + i % 2][0:T, 0:HR * T] for i in range(ROUNDS)]
        ps_z1T = banks[4][:, 0:VGROUPS * T]
        ps_y1 = banks[3][0:T, 0:D]
        ps_slot2T = [banks[5 + i % 2][:, 0:HR * T] for i in range(4)]
        ps_s2 = [banks[5 + i % 2][0:T, 0:HR * T] for i in range(ROUNDS)]
        ps_pT = [banks[7 - i % 2][0:T, 0:HR * T] for i in range(ROUNDS)]
        ps_zsT = banks[6][:, 0:VGROUPS * T]

        weights_in = sem("weights_in")
        consts_in = sem("consts_in")
        slots_in = sem("slots_in")
        zeros_set = sem("zeros_set")
        fills_set = sem("fills_set")
        rope_set = sem("rope_set")
        x_in = [sem(f"x_in{i}") for i in range(2)]
        out_stored = sem("out_stored")
        tok_done = sem("tok_done")
        h0_set = sem("h0_set")
        stat0_set = sem("stat0_set")
        mv0_set = sem("mv0_set")
        var0_set = sem("var0_set")
        rstd0_set = sem("rstd0_set")
        xn_set = sem("xn_set")
        xnT_done = sem("xnT_done")
        xnT_copied = sem("xnT_copied")
        qk1_done = sem("qk1_done")
        v1_done = sem("v1_done")
        qk1_copied = sem("qk1_copied")
        v1_copied = sem("v1_copied")
        sq_set = sem("sq_set")
        ss_set = sem("ss_set")
        ms_set = sem("ms_set")
        rms_set = sem("rms_set")
        qkn_set = sem("qkn_set")
        own_set = sem("own_set")
        other_set = sem("other_set")
        qkr_set = sem("qkr_set")
        high1_set = sem("high1_set")
        slot1_set = sem("slot1_set")
        slot1T_done = [sem(f"slot1T_done{i}") for i in range(4)]
        slot1T_copied = [sem(f"slot1T_copied{i}") for i in range(4)]
        s1_done = [sem(f"s1_done{i}") for i in range(ROUNDS)]
        square_set = [sem(f"square_set{i}") for i in range(ROUNDS)]
        pat_set = [sem(f"pat_set{i}") for i in range(ROUNDS)]
        z1T_done = sem("z1T_done")
        z1T_copied = sem("z1T_copied")
        y1_done = sem("y1_done")
        h1_set = sem("h1_set")
        h1b_set = sem("h1b_set")
        stat1_set = sem("stat1_set")
        mv1_set = sem("mv1_set")
        var1_set = sem("var1_set")
        rstd1_set = sem("rstd1_set")
        xc_set = sem("xc_set")
        x2T_done = sem("x2T_done")
        x2T_copied = sem("x2T_copied")
        gate_done = sem("gate_done")
        nmax_set = sem("nmax_set")
        ex_set = sem("ex_set")
        rsum_set = sem("rsum_set")
        scale_set = sem("scale_set")
        top_set = sem("top_set")
        top2_set = sem("top2_set")
        rest_set = sem("rest_set")
        picked_set = sem("picked_set")
        combine_set = sem("combine_set")
        hw_set = sem("hw_set")
        catT_done = sem("catT_done")
        catT_copied = sem("catT_copied")
        qk2_done = sem("qk2_done")
        v2_done = sem("v2_done")
        high2_set = sem("high2_set")
        slot2_set = sem("slot2_set")
        v2_copied = sem("v2_copied")
        slot2T_done = [sem(f"slot2T_done{i}") for i in range(4)]
        slot2T_copied = [sem(f"slot2T_copied{i}") for i in range(4)]
        s2_done = [sem(f"s2_done{i}") for i in range(ROUNDS)]
        smax_set = [sem(f"smax_set{i}") for i in range(ROUNDS)]
        shift_set = [sem(f"shift_set{i}") for i in range(ROUNDS)]
        prob_set = [sem(f"prob_set{i}") for i in range(ROUNDS)]
        pT_done = [sem(f"pT_done{i}") for i in range(ROUNDS)]
        pT_copied = [sem(f"pT_copied{i}") for i in range(ROUNDS)]
        zsT_done = sem("zsT_done")
        zsT_copied = sem("zsT_copied")
        zs_done = sem("zs_done")
        rden_set = sem("rden_set")
        z2_set = sem("z2_set")
        z2T_done = sem("z2T_done")
        z2T_copied = sem("z2T_copied")
        y2_done = sem("y2_done")
        out_set = sem("out_set")

        WEIGHTS = 12
        CONSTS = 5

        class Step:

            def __init__(self, eng, n, parity):
                self.eng, self.n, self.parity = eng, n, parity
                self.fixed = isinstance(n, int)

            def other(self, by):
                return Step(self.eng, self.n + by, (self.parity + by) % 2)

            def works(self, stage):
                return not self.fixed or 0 <= self.n - stage < TILES

            def par(self, stage):
                return (self.parity + stage) % 2

            def began(self, stage, back=0):
                return not self.fixed or self.n - stage - back >= 0

            def upto(self, stage, back=0):
                count = self.n - stage + (1 - back)
                return min(count, TILES) if self.fixed else count

            def patches(self):
                return self.n * 8 + (16 - 8 * self.parity)

        FIRST = 6
        STEPS = TILES + STAGES - 1

        def run(eng, step):
            for n in range(-1, FIRST):
                step(Step(eng, n, n % 2))
            with eng.Fori(FIRST, TILES, 2) as n:
                step(Step(eng, n, 0))
                step(Step(eng, n + 1, 1))
            for n in range(TILES, STEPS + 1):
                step(Step(eng, n, n % 2))

        block = ctx.enter_context(nc.Block())

        @block.sync
        def _(sp):
            sp.dma_start(tok_w[:, :, :], w_tok).then_inc(weights_in, 16)
            for dst, src in ((tok_b, b_tok.broadcast_to([T, D])), (ident, identity)):
                sp.dma_start(dst[:, :], src).then_inc(consts_in, 16)
            sp.dma_start(x_sb[0][:, :, :], x_tiles[0]).then_inc(x_in[0], 16)
            for dst, src in ((qkv1_w0, w_qkv1[0:P]), (qkv1_w1, w_qkv1[P:D + 1])):
                sp.dma_start(dst[:, :], src).then_inc(weights_in, 16)
            sp.dma_start(x_sb[1][:, :, :], x_tiles[1]).then_inc(x_in[1], 16)
            for dst, src in ((gate_w0, w_gate[0:P]),
                             (gate_w1, w_gate[P:D + 1]), (qkv2_w0, w_qkv2[0:P]),
                             (qkv2_w1, w_qkv2[P:D + 1 + E]), (lora_w, w_lora),
                             (proj_w0, w_proj[0:P]), (proj_w1, w_proj[P:D]),
                             (proj_b, b_proj.broadcast_to([T, D]))):
                sp.dma_start(dst[:, :], src).then_inc(weights_in, 16)
            sp.dma_start(o1_w[:, :, :], w_o1).then_inc(weights_in, 16)

            x_pairs = x_tiles.rearrange("(m k) p c t -> m k p c t", k=2)
            out_pairs = out.rearrange("(m k) t d -> m k t d", k=2)

            def load(m, k):
                sp.wait_ge(tok_done, 2 * m + (k - 1))
                sp.dma_start(x_sb[k][:, :, :], x_pairs[m, k]).then_inc(x_in[k], 16)

            def store(m, k):
                sp.wait_ge(out_set, 2 * m + (k + 1))
                sp.dma_start(out_pairs[m, k], out_sb[k][:, :]).then_inc(out_stored, 16)

            for n in range(2, FIRST):
                load(n // 2, n % 2)
            with sp.Fori(FIRST // 2, TILES // 2) as m:
                for k in range(2):
                    load(m, k)
                    store(m - FIRST // 2, k)
            for t in range(TILES - FIRST, TILES):
                store(t // 2, t % 2)
            sp.wait_ge(out_stored, 16 * TILES)

        @block.tensor
        def _(pe):
            def transpose(dst, src):
                n = src.shape[0]
                return nc.tensor.transpose(dst, src, ident[0:n, 0:n])

            def tokens(s):
                pe.wait_ge(x_in[s.parity], s.patches())
                if s.began(0, 1):
                    pe.wait_ge(xnT_copied, s.upto(0, 1))
                if s.began(4):
                    pe.wait_ge(z2_set, s.upto(4))
                for c in range(CK // 2):
                    nc.tensor.matmul(ps_tok, x_sb[s.par(0)][:, c, :], tok_w[:, c, :],
                                     start=(c == 0), stop=False)

            def tokens_end(s):
                for c in range(CK // 2, CK):
                    mm = nc.tensor.matmul(ps_tok, x_sb[s.par(0)][:, c, :], tok_w[:, c, :],
                                          start=False, stop=(c == CK - 1))
                mm.then_inc(tok_done, 1)

            def turn_xn(s):
                pe.wait_ge(xn_set, s.upto(0))
                if s.began(4):
                    pe.wait_ge(out_set, s.upto(4))
                for c in range(2):
                    mm = transpose(ps_xnT[:, c * T:(c + 1) * T], xn[:, c * P:(c + 1) * P])
                mm.then_inc(xnT_done, 1)

            def project_qk1(s):
                pe.wait_ge(xnT_copied, s.upto(0))
                if s.began(2, 1):
                    pe.wait_ge(slot2_set, s.upto(2, 1))
                if s.began(2):
                    pe.wait_ge(hw_set, s.upto(2))
                c = slice(0, 2 * D)
                nc.tensor.matmul(ps_qk1, xnT[:, 0, :], qkv1_w0[:, c], start=True, stop=False)
                nc.tensor.matmul(ps_qk1, xnT[0:D2 + 1, 1, :], qkv1_w1[:, c],
                                 start=False, stop=True).then_inc(qk1_done, 1)

            def project_v1(s):
                pe.wait_ge(xnT_copied, s.upto(0))
                if s.began(2):
                    pe.wait_ge(x2T_copied, s.upto(2))
                c = slice(2 * D, 3 * D)
                nc.tensor.matmul(ps_v1, xnT[:, 0, :], qkv1_w0[:, c], start=True, stop=False)
                nc.tensor.matmul(ps_v1, xnT[0:D2 + 1, 1, :], qkv1_w1[:, c],
                                 start=False, stop=True).then_inc(v1_done, 1)

            def turn_slot1(s, i):
                if i < 2:
                    pe.wait_ge(slot1_set, s.upto(1))
                if i == 0:
                    if s.began(1, 1):
                        pe.wait_ge(h1_set, s.upto(1, 1))
                elif i == 1:
                    if s.began(1, 1):
                        pe.wait_ge(z1T_copied, s.upto(1, 1))
                else:
                    pe.wait_ge(slot1T_copied[i - 2], s.upto(1))
                for g in range(HR):
                    p = i % 2 * H + STRIPS * (i // 2 * HR + g)
                    src = slot1[:, p:p + STRIPS, :].bitcast(fp32).rearrange("t h d -> t (h d)")
                    mm = transpose(ps_slot1T[i][:, g * T:(g + 1) * T], src)
                mm.then_inc(slot1T_done[i], 1)

            def scores1(s, i):
                pe.wait_ge(slot1T_copied[i // 2 * 2], s.upto(1))
                pe.wait_ge(slot1T_copied[i // 2 * 2 + 1], s.upto(1))
                if i < 2:
                    pe.wait_ge(slot1T_copied[i + 2], s.upto(1))
                else:
                    pe.wait_ge(square_set[i - 2], s.upto(1))
                r = slice(i % 2 * SLOT, i % 2 * SLOT + SPLIT)
                for g in range(HR):
                    mm = nc.tensor.matmul(ps_s1[i][:, g * T:(g + 1) * T], qk1T[r, 1, i // 2 * HR + g, :],
                                          qk1T[r, 0, i // 2 * HR + g, :], start=True, stop=True)
                mm.then_inc(s1_done[i], 1)

            def values1(s):
                pe.wait_ge(square_set[3], s.upto(1))
                for i in range(ROUNDS):
                    pe.wait_ge(pat_set[i], s.upto(1))
                    for h in range(i * HR, (i + 1) * HR):
                        g, j = h // VSTRIPS, h % VSTRIPS
                        mm = nc.tensor.matmul(ps_z1T[j * VSLOT:(j + 1) * VSLOT, g * T:(g + 1) * T],
                                              v1[s.par(1)][:, h, :], pat[:, h, :],
                                              start=True, stop=True)
                mm.then_inc(z1T_done, 1)

            def output1(s):
                pe.wait_ge(z1T_copied, s.upto(1))
                pe.wait_ge(square_set[2], s.upto(1))
                for g in range(VGROUPS):
                    mm = nc.tensor.matmul(ps_y1, z1T[:, g, :], o1_w[:, g, :],
                                          start=(g == 0), stop=(g == VGROUPS - 1))
                mm.then_inc(y1_done, 1)

            def turn_x2(s):
                pe.wait_ge(xc_set, s.upto(2))
                if s.began(2, 1):
                    pe.wait_ge(catT_copied, s.upto(2, 1))
                pe.wait_ge(v1_copied, s.upto(1))
                for c in range(2):
                    mm = transpose(ps_x2T[:, c * T:(c + 1) * T], xc[:, c * P:(c + 1) * P])
                mm.then_inc(x2T_done, 1)

            def gate(s):
                pe.wait_ge(x2T_copied, s.upto(2))
                if s.began(2, 1):
                    pe.wait_ge(slot2_set, s.upto(2, 1))
                pe.wait_ge(qk1_copied, s.upto(1))
                nc.tensor.matmul(ps_gate, x2T[:, 0, :], gate_w0[:, :], start=True, stop=False)
                nc.tensor.matmul(ps_gate, x2T[0:D2 + 1, 1, :], gate_w1[:, :],
                                 start=False, stop=True).then_inc(gate_done, 1)

            def turn_cat(s):
                pe.wait_ge(combine_set, s.upto(2))
                pe.wait_ge(hw_set, s.upto(2))
                pe.wait_ge(v1_copied, s.upto(0))
                transpose(ps_x2T[:, 0:T], xc[:, P:2 * P])
                transpose(ps_x2T[:, T:2 * T], hw[:, :, :].rearrange("t e r -> t (e r)"))\
                    .then_inc(catT_done, 1)

            def project_qk2(s):
                pe.wait_ge(catT_copied, s.upto(2))
                pe.wait_ge(qk1_copied, s.upto(0))
                c = slice(0, 2 * D)
                nc.tensor.matmul(ps_qk2, x2T[:, 0, :], qkv2_w0[:, c], start=True, stop=False)
                nc.tensor.matmul(ps_qk2, catT[0:D2 + 1 + E, 0, :], qkv2_w1[:, c],
                                 start=False, stop=False)
                nc.tensor.matmul(ps_qk2, catT[:, 1, :], lora_w[:, c],
                                 start=False, stop=True).then_inc(qk2_done, 1)

            def project_v2(s):
                pe.wait_ge(catT_copied, s.upto(2))
                if s.began(3):
                    pe.wait_ge(pT_copied[0], s.upto(3))
                c = slice(2 * D, 3 * D)
                nc.tensor.matmul(ps_v2, x2T[:, 0, :], qkv2_w0[:, c], start=True, stop=False)
                nc.tensor.matmul(ps_v2, catT[0:D2 + 1 + E, 0, :], qkv2_w1[:, c],
                                 start=False, stop=False)
                nc.tensor.matmul(ps_v2, catT[:, 1, :], lora_w[:, c],
                                 start=False, stop=True).then_inc(v2_done, 1)

            def turn_slot2(s, i):
                if i < 2:
                    pe.wait_ge(slot2_set, s.upto(3))
                if i == 1:
                    if s.began(3, 1):
                        pe.wait_ge(zsT_copied, s.upto(3, 1))
                elif i > 1:
                    pe.wait_ge(slot2T_copied[i - 2], s.upto(3))
                for g in range(HR):
                    p = i % 2 * H + STRIPS * (i // 2 * HR + g)
                    src = slot2[:, p:p + STRIPS, :].bitcast(fp32).rearrange("t h d -> t (h d)")
                    mm = transpose(ps_slot2T[i][:, g * T:(g + 1) * T], src)
                mm.then_inc(slot2T_done[i], 1)

            def scores2(s, i):
                pe.wait_ge(slot2T_copied[i // 2 * 2], s.upto(3))
                pe.wait_ge(slot2T_copied[i // 2 * 2 + 1], s.upto(3))
                if i < 2:
                    pe.wait_ge(slot2T_copied[i + 2], s.upto(3))
                else:
                    pe.wait_ge(shift_set[i - 2], s.upto(3))
                r = slice(i % 2 * SLOT, i % 2 * SLOT + KX)
                for g in range(HR):
                    mm = nc.tensor.matmul(ps_s2[i][:, g * T:(g + 1) * T], qk2T[r, 0, i // 2 * HR + g, :],
                                          qk2T[r, 1, i // 2 * HR + g, :], start=True, stop=True)
                mm.then_inc(s2_done[i], 1)

            def turn_prob(s, i):
                pe.wait_ge(prob_set[i], s.upto(3))
                if i == 0:
                    pe.wait_ge(v2_copied, s.upto(3))
                elif i == 1:
                    pe.wait_ge(shift_set[3], s.upto(3))
                else:
                    pe.wait_ge(pT_copied[i - 2], s.upto(3))
                    if i == 2 and s.works(2):
                        pe.wait_ge(v2_copied, s.upto(2))
                for g in range(HR):
                    mm = transpose(ps_pT[i][:, g * T:(g + 1) * T], prob[:, i * HR + g, :])
                mm.then_inc(pT_done[i], 1)

            def values2(s):
                pe.wait_ge(pT_copied[3], s.upto(3))
                for i in range(ROUNDS):
                    pe.wait_ge(pT_copied[i], s.upto(3))
                    for h in range(i * HR, (i + 1) * HR):
                        g, j = h // VSTRIPS, h % VSTRIPS
                        mm = nc.tensor.matmul(ps_zsT[j * VSLOT:(j + 1) * VSLOT, g * T:(g + 1) * T],
                                              v2[s.par(3)][:, h, :], probT[:, h, :],
                                              start=True, stop=True)
                mm.then_inc(zsT_done, 1)

            def turn_zs(s):
                pe.wait_ge(zsT_copied, s.upto(4))
                pe.wait_ge(xnT_copied, s.upto(0, 1))
                for g in range(VGROUPS):
                    mm = transpose(ps_zs[:, g * P:(g + 1) * P], zsT[:, g, :])
                mm.then_inc(zs_done, 1)

            def turn_z2(s):
                pe.wait_ge(z2_set, s.upto(4))
                pe.wait_ge(h0_set, s.upto(0))
                z = z2[:, :, :].rearrange("t h d -> t (h d)")
                transpose(ps_z2T[:, 0:T], z[:, 0:P])
                transpose(ps_z2T[0:D2, T:2 * T], z[:, P:D]).then_inc(z2T_done, 1)

            def output2(s):
                pe.wait_ge(z2T_copied, s.upto(4))
                nc.tensor.matmul(ps_y2, z2T[:, 0, :], proj_w0[:, :], start=True, stop=False)
                nc.tensor.matmul(ps_y2, z2T[0:D2, 1, :], proj_w1[:, :],
                                 start=False, stop=True).then_inc(y2_done, 1)

            def step(s):
                s0, s1, s2, s3, s4 = (s.works(k) for k in range(STAGES))
                ahead = s.other(1)
                behind = s.other(-1)
                if behind.works(3): values2(behind)
                if s3: turn_slot2(s, 2); turn_slot2(s, 1)
                if s4: turn_zs(s)
                if s3: turn_slot2(s, 3); scores2(s, 0)
                if s0: tokens(s); tokens_end(s)
                if s2: turn_x2(s)
                if s1: turn_slot1(s, 1); turn_slot1(s, 0)
                if s4: turn_z2(s)
                if s2: gate(s)
                if s1: turn_slot1(s, 3)
                if s4: output2(s)
                if s1: turn_slot1(s, 2); scores1(s, 1)
                if s3: turn_prob(s, 0)
                if s0: turn_xn(s)
                if s3: scores2(s, 2)
                if s1: scores1(s, 0)
                if s3: scores2(s, 1)
                if s1: scores1(s, 3)
                if s0: project_v1(s)
                if s1: scores1(s, 2)
                if s0: project_qk1(s)
                if s3: scores2(s, 3)
                if s2: turn_cat(s)
                if s1: values1(s)
                if s2: project_qk2(s)
                if s3: turn_prob(s, 1)
                if s2: project_v2(s)
                if s3: turn_prob(s, 3)
                if s1: output1(s)
                if s3: turn_prob(s, 2)
                if ahead.works(3): turn_slot2(ahead, 0)

            pe.wait_ge(weights_in, 16 * WEIGHTS)
            pe.wait_ge(consts_in, 16 * CONSTS)
            run(pe, step)

        @block.scalar
        def _(act):
            copy = nc.scalar.copy

            def copy_xnT(s):
                act.wait_ge(xnT_done, s.upto(0))
                copy(xnT[:, :, :], ps_xnT.rearrange("p (c t) -> p c t", c=2)).then_inc(xnT_copied, 1)

            def copy_qk1(s):
                act.wait_ge(qk1_done, s.upto(0))
                if s.began(0, 2):
                    act.wait_ge(qkn_set, s.upto(0, 2))
                copy(qk1[s.par(0)][:, :, :].rearrange("t h d -> t (h d)"), ps_qk1).then_inc(qk1_copied, 1)

            def copy_v1(s):
                act.wait_ge(v1_done, s.upto(0))
                if s.began(0, 2):
                    act.wait_ge(z1T_done, s.upto(0, 2))
                copy(v1[s.par(0)][:, :, 0:DH], ps_v1.rearrange("t (h d) -> t h d", d=DH)).then_inc(v1_copied, 1)

            def high_parts(slot, src, out_sem):
                q, k = slot[:, 0:H, :], slot[:, H:2 * H, :]
                for dst, part in ((q[:, :, 0:DH], 0), (q[:, :, 2 * DH:3 * DH], 0),
                                  (k[:, :, 0:DH], 1), (k[:, :, DH:2 * DH], 1)):
                    op = copy(dst, src[:, part * H:(part + 1) * H, :])
                op.then_inc(out_sem, 1)

            def high1(s):
                act.wait_ge(qkr_set, s.upto(0))
                if s.began(0, 1):
                    act.wait_ge(slot1T_done[2], s.upto(0, 1))
                    act.wait_ge(slot1T_done[3], s.upto(0, 1))
                high_parts(slot1, qkr[:, :, :], high1_set)

            def copy_slot1T(s, i):
                act.wait_ge(slot1T_done[i], s.upto(1))
                copy(qk1T[:, i % 2, i // 2 * HR:(i // 2 + 1) * HR, :],
                     ps_slot1T[i].rearrange("p (g t) -> p g t", g=HR)).then_inc(slot1T_copied[i], 1)

            def squares(s, g):
                act.wait_ge(s1_done[g], s.upto(1))
                if g < 2:
                    if s.began(1, 1):
                        act.wait_ge(z1T_done, s.upto(1, 1))
                nc.scalar.activation(pat[:, g * HR:(g + 1) * HR, :],
                                     ps_s1[g].rearrange("t (h k) -> t h k", h=HR),
                                     ACT.Square, scale=1.0 / DH).then_inc(square_set[g], 1)

            def copy_z1T(s):
                act.wait_ge(z1T_done, s.upto(1))
                copy(z1T[:, :, :], ps_z1T.rearrange("p (g t) -> p g t", g=VGROUPS)).then_inc(z1T_copied, 1)

            def copy_x2T(s):
                act.wait_ge(x2T_done, s.upto(2))
                if s.began(2, 1):
                    act.wait_ge(qk2_done, s.upto(2, 1))
                if s.began(2, 1):
                    act.wait_ge(v2_done, s.upto(2, 1))
                copy(x2T[:, :, :], ps_x2T.rearrange("p (c t) -> p c t", c=2)).then_inc(x2T_copied, 1)

            def router_exp(s):
                act.wait_ge(nmax_set, s.upto(2))
                if s.began(2, 1):
                    act.wait_ge(picked_set, s.upto(2, 1))
                nc.scalar.activation(ex[:, 0:E], ps_gate[:, R:R + E], ACT.Exp, bias=nmax[:, 0:1],
                                     accum_out=exsum[:, 0:1]).then_inc(ex_set, 1)

            def copy_catT(s):
                act.wait_ge(catT_done, s.upto(2))
                copy(catT[:, :, :], ps_x2T.rearrange("p (c t) -> p c t", c=2)).then_inc(catT_copied, 1)

            def high2(s):
                act.wait_ge(qk2_done, s.upto(2))
                if s.began(3):
                    act.wait_ge(slot2T_done[2], s.upto(3))
                    act.wait_ge(slot2T_done[3], s.upto(3))
                high_parts(slot2, ps_qk2.rearrange("t (h d) -> t h d", d=DH), high2_set)

            def copy_v2(s):
                act.wait_ge(v2_done, s.upto(2))
                if s.began(2, 2):
                    act.wait_ge(zsT_done, s.upto(2, 2))
                copy(v2[s.par(2)][:, :, 0:DH], ps_v2.rearrange("t (h d) -> t h d", d=DH))\
                    .then_inc(v2_copied, 1)

            def copy_slot2T(s, i):
                act.wait_ge(slot2T_done[i], s.upto(3))
                copy(qk2T[:, i % 2, i // 2 * HR:(i // 2 + 1) * HR, :],
                     ps_slot2T[i].rearrange("p (g t) -> p g t", g=HR)).then_inc(slot2T_copied[i], 1)

            def probs(s, g):
                act.wait_ge(shift_set[g], s.upto(3))
                heads = prob[:, g * HR:(g + 1) * HR, :]
                nc.scalar.activation(heads, heads, ACT.Exp, scale=SM_SCALE).then_inc(prob_set[g], 1)

            def copy_probT(s, g):
                act.wait_ge(pT_done[g], s.upto(3))
                if g == 0:
                    if s.began(3, 1):
                        act.wait_ge(zsT_done, s.upto(3, 1))
                copy(probT[:, g * HR:(g + 1) * HR, :],
                     ps_pT[g].rearrange("t (h k) -> t h k", h=HR)).then_inc(pT_copied[g], 1)

            def copy_zsT(s):
                act.wait_ge(zsT_done, s.upto(3))
                if s.began(3, 1):
                    act.wait_ge(zs_done, s.upto(3, 1))
                copy(zsT[:, :, :], ps_zsT.rearrange("p (g t) -> p g t", g=VGROUPS)).then_inc(zsT_copied, 1)

            def copy_z2T(s):
                act.wait_ge(z2T_done, s.upto(4))
                copy(z2T[:, 0, :], ps_z2T[:, 0:T])
                copy(z2T[0:D2, 1, :], ps_z2T[0:D2, T:2 * T]).then_inc(z2T_copied, 1)

            def step(s):
                s0, s1, s2, s3, s4 = (s.works(k) for k in range(STAGES))
                ahead = s.other(1)
                behind = s.other(-1)
                if s3: copy_slot2T(s, 1); copy_slot2T(s, 2)
                if behind.works(0): high1(behind)
                if s2: copy_x2T(s)
                if s4: copy_z2T(s)
                if s1: copy_slot1T(s, 0)
                if s2: router_exp(s)
                if s3: probs(s, 0); copy_slot2T(s, 3)
                if s1: copy_slot1T(s, 2); squares(s, 1)
                if s0: copy_xnT(s)
                if s1: squares(s, 0)
                if s0: copy_v1(s)
                if s1: squares(s, 2); squares(s, 3)
                if s0: copy_qk1(s)
                if s2: copy_catT(s)
                if s3: probs(s, 1)
                if s1: copy_z1T(s)
                if s3: copy_probT(s, 0); probs(s, 3)
                if s2: high2(s); copy_v2(s)
                if s3: probs(s, 2); copy_probT(s, 2)
                if ahead.works(3): copy_slot2T(ahead, 0)
                if s3: copy_zsT(s)

            act.dma_start(g_sb[:, :], g_rows.broadcast_to([T, 2 * DH])).then_inc(consts_in, 16)
            act.dma_start(rope_sb[:, :], rope_rows).then_inc(consts_in, 16)
            act.dma_start(keep[:, :], causal_keep).then_inc(consts_in, 16)
            for i in range(2):
                act.dma_start(slot2[:, i * H:(i + 1) * H, SPLIT:SLOT].bitcast(fp32), image_rows[:, i]).then_inc(slots_in, 16)
            act.wait_ge(zeros_set, 8)
            act.wait_ge(slots_in, 16 * 2)
            run(act, step)

        @block.vector
        def _(dve):
            def embed(s):
                dve.wait_ge(tok_done, s.upto(0))
                if s.began(0, 2):
                    dve.wait_ge(h1_set, s.upto(0, 2))
                if s.began(0, 1):
                    dve.wait_ge(xn_set, s.upto(0, 1))
                nc.vector.tensor_tensor(h0[s.par(0)][:, :], ps_tok, tok_b[:, :], ALU.add).then_inc(h0_set, 1)

            def stats(s, stage, src, src_sem, stat, stat_sem):
                dve.wait_ge(src_sem, s.upto(stage))
                nc.vector.bn_stats(stat[:, :], src[:, :]).then_inc(stat_sem, 1)
                dve.wait_ge(stat_sem, s.upto(stage))

            def moments(mv, stat, mv_sem):
                nc.vector.bn_aggr(mv[:, :], stat[:, :]).then_inc(mv_sem, 1)

            def variance(s, stage, mv, mv_sem, var, var_sem):
                dve.wait_ge(mv_sem, s.upto(stage))
                nc.vector.tensor_scalar(var[:, :], mv[:, 1:2], LN_EPS, None, ALU.add).then_inc(var_sem, 1)

            def stats0(s):
                stats(s, 0, h0[s.par(0)], h0_set, stat0, stat0_set)

            def moments0(s):
                moments(mv0, stat0, mv0_set)
                variance(s, 0, mv0, mv0_set, var0, var0_set)

            def stats1(s):
                stats(s, 1, h1[s.par(1)], h1_set, stat1, stat1_set)

            def moments1(s):
                moments(mv1, stat1, mv1_set)
                variance(s, 1, mv1, mv1_set, var1, var1_set)

            def normalize0(s):
                dve.wait_ge(rstd0_set, s.upto(0))
                if s.began(0, 1):
                    dve.wait_ge(xnT_done, s.upto(0, 1))
                nc.vector.tensor_scalar(xn[:, 0:D], h0[s.par(0)][:, :], mv0[:, 0:1], rstd0[:, 0:1],
                                        ALU.subtract, ALU.mult).then_inc(xn_set, 1)

            def normalize1(s):
                dve.wait_ge(rstd1_set, s.upto(1))
                if s.began(1, 1):
                    dve.wait_ge(catT_done, s.upto(1, 1))
                nc.vector.tensor_scalar(xc[:, 0:D], h1[s.par(1)][:, :], mv1[:, 0:1], rstd1[:, 0:1],
                                        ALU.subtract, ALU.mult).then_inc(xc_set, 1)

            def head_sums(s):
                dve.wait_ge(sq_set, s.upto(0))
                nc.vector.tensor_reduce(ss[:, :], sq[:, :, :], AX.X, ALU.add).then_inc(ss_set, 1)
                dve.wait_ge(ss_set, s.upto(0))
                nc.vector.tensor_scalar(ms[:, :], ss[:, :], 1.0 / DH, RMS_EPS, ALU.mult, ALU.add)\
                    .then_inc(ms_set, 1)

            def head_norm(s):
                dve.wait_ge(rms_set, s.upto(0))
                if s.began(0, 1):
                    dve.wait_ge(own_set, s.upto(0, 1))
                nc.vector.tensor_tensor(qkn[:, :, :], qk1[s.par(0)][:, :, :],
                                        rms[:, :].unsqueeze(2).broadcast_to([T, 2 * H, DH]),
                                        ALU.mult).then_inc(qkn_set, 1)

            def rotate(s):
                dve.wait_ge(qkn_set, s.upto(0))
                if s.began(0, 1):
                    dve.wait_ge(qkr_set, s.upto(0, 1))
                for i in range(2):
                    dst = slice(i * HALF, (i + 1) * HALF)
                    src = slice((1 - i) * HALF, (2 - i) * HALF)
                    table = rope[:, DH + i * HALF:DH + (i + 1) * HALF].unsqueeze(1)
                    op = nc.vector.tensor_tensor(other[:, :, dst], qkn[:, :, src],
                                                 table.broadcast_to([T, 2 * H, HALF]), ALU.mult)
                op.then_inc(other_set, 1)

            def add_halves(s):
                dve.wait_ge(other_set, s.upto(0))
                dve.wait_ge(own_set, s.upto(0))
                if s.began(0, 1):
                    dve.wait_ge(high1_set, s.upto(0, 1))
                nc.vector.tensor_tensor(qkr[:, :, :], own[:, :, :], other[:, :, :], ALU.add)\
                    .then_inc(qkr_set, 1)

            def low_parts(slot, src):
                for i in range(2):
                    heads = slice(i * H, (i + 1) * H)
                    op = nc.vector.tensor_tensor(
                        slot[:, heads, (i + 1) * DH:(i + 2) * DH], src[:, heads, :],
                        slot[:, heads, 0:DH].bitcast(fp32), ALU.subtract)
                return op

            def low1(s):
                dve.wait_ge(high1_set, s.upto(0))
                low_parts(slot1, qkr[:, :, :]).then_inc(slot1_set, 1)

            def low2(s):
                dve.wait_ge(high2_set, s.upto(2))
                low_parts(slot2, ps_qk2.rearrange("t (h d) -> t h d", d=DH)).then_inc(slot2_set, 1)

            def residual1(s):
                dve.wait_ge(y1_done, s.upto(1))
                if s.began(1, 2):
                    dve.wait_ge(xc_set, s.upto(1, 2))
                if s.began(1, 2):
                    dve.wait_ge(h1b_set, s.upto(1, 2))
                nc.vector.tensor_tensor(h1[s.par(1)][:, :], ps_y1, h0[s.par(1)][:, :], ALU.add)\
                    .then_inc(h1_set, 1)

            def router_max(s):
                dve.wait_ge(gate_done, s.upto(2))
                nc.vector.tensor_reduce(nmax[:, :], ps_gate[:, R:R + E], AX.X, ALU.max, negate=True)\
                    .then_inc(nmax_set, 1)

            def route(s):
                dve.wait_ge(ex_set, s.upto(2))
                nc.vector.reciprocal(rsum[:, :], exsum[:, :]).then_inc(rsum_set, 1)
                nc.vector.max(top[:, :], ex[:, 0:E]).then_inc(top_set, 1)
                dve.wait_ge(top_set, s.upto(2))
                nc.vector.tensor_copy(top2[:, 0:2], top[:, 0:2]).then_inc(top2_set, 1)
                dve.wait_ge(rsum_set, s.upto(2))
                dve.wait_ge(top2_set, s.upto(2))
                nc.vector.tensor_scalar(lora_scale[:, :], rsum[:, :], LORA_SCALE, None, ALU.mult)\
                    .then_inc(scale_set, 1)
                nc.vector.match_replace(rest[:, :], top2[:, :], ex[:, :], 0.0).then_inc(rest_set, 1)
                dve.wait_ge(rest_set, s.upto(2))
                nc.vector.tensor_tensor(picked[:, :], ex[:, 0:E], rest[:, 0:E], ALU.subtract)\
                    .then_inc(picked_set, 1)
                dve.wait_ge(picked_set, s.upto(2))
                dve.wait_ge(scale_set, s.upto(2))
                dve.wait_ge(x2T_done, s.upto(2))
                nc.vector.tensor_scalar(xc[:, D + 1:D + 1 + E], picked[:, :], lora_scale[:, 0:1], None,
                                        ALU.mult).then_inc(combine_set, 1)
                dve.wait_ge(combine_set, s.upto(2))
                nc.vector.tensor_tensor(
                    hw[:, :, :], ps_gate[:, 0:R].rearrange("t (e r) -> t e r", e=E),
                    xc[:, D + 1:D + 1 + E].unsqueeze(2).broadcast_to([T, E, RANK]),
                    ALU.mult).then_inc(hw_set, 1)

            def shift(s, g):
                dve.wait_ge(s2_done[g], s.upto(3))
                heads = slice(g * HR, (g + 1) * HR)
                scores = ps_s2[g].rearrange("t (h k) -> t h k", h=HR)
                nc.vector.tensor_reduce(smax[:, heads], scores, AX.X, ALU.max).then_inc(smax_set[g], 1)
                dve.wait_ge(smax_set[g], s.upto(3))
                if s.began(3, 1):
                    dve.wait_ge(pT_done[g], s.upto(3, 1))
                nc.vector.tensor_tensor(prob[:, heads, :], scores,
                                        smax[:, heads].unsqueeze(2).broadcast_to([T, HR, T]),
                                        ALU.subtract).then_inc(shift_set[g], 1)

            def copy_slot1T(s, i):
                dve.wait_ge(slot1T_done[i], s.upto(1))
                nc.vector.tensor_copy(qk1T[:, i % 2, i // 2 * HR:(i // 2 + 1) * HR, :],
                                      ps_slot1T[i].rearrange("p (g t) -> p g t", g=HR))\
                    .then_inc(slot1T_copied[i], 1)

            def mask(s, g):
                dve.wait_ge(square_set[g], s.upto(1))
                heads = pat[:, g * HR:(g + 1) * HR, :]
                nc.vector.tensor_tensor(heads, heads, keep[:, :].unsqueeze(1).broadcast_to([T, HR, T]),
                                        ALU.mult).then_inc(pat_set[g], 1)

            def copy_probT(s, g):
                dve.wait_ge(pT_done[g], s.upto(3))
                if g == 1:
                    if s.began(3, 1):
                        dve.wait_ge(zsT_done, s.upto(3, 1))
                nc.vector.tensor_copy(probT[:, g * HR:(g + 1) * HR, :],
                                      ps_pT[g].rearrange("t (h k) -> t h k", h=HR))\
                    .then_inc(pT_copied[g], 1)

            def divide(s):
                dve.wait_ge(zs_done, s.upto(4))
                z = ps_zs.rearrange("t (h d) -> t h d", d=VSLOT)
                nc.vector.reciprocal(rden[:, :], z[:, :, DH]).then_inc(rden_set, 1)
                dve.wait_ge(rden_set, s.upto(4))
                nc.vector.tensor_tensor(z2[:, :, :], z[:, :, 0:DH],
                                        rden[:, :].unsqueeze(2).broadcast_to([T, H, DH]),
                                        ALU.mult).then_inc(z2_set, 1)

            def residual2(s):
                dve.wait_ge(y2_done, s.upto(4))
                dve.wait_ge(h1b_set, s.upto(4))
                if s.began(4, 1):
                    dve.wait_ge(out_stored, s.upto(4, 1) * 16)
                nc.vector.tensor_tensor(out_sb[s.par(4)][:, :], ps_y2, h1b[s.par(4)][:, :], ALU.add)\
                    .then_inc(out_set, 1)

            def step(s):
                s0, s1, s2, s3, s4 = (s.works(k) for k in range(STAGES))
                ahead = s.other(1)
                behind = s.other(-1)
                if s3: shift(s, 0)
                if behind.works(0): low1(behind)
                if s0: embed(s); stats0(s)
                if s1: copy_slot1T(s, 1)
                if s0: moments0(s)
                if s2: router_max(s)
                if s1: copy_slot1T(s, 3)
                if s0: normalize0(s)
                if s4: residual2(s)
                if s2: route(s)
                if s3: shift(s, 1); shift(s, 2)
                if s1: mask(s, 3)
                if s3: shift(s, 3)
                if s0: head_sums(s)
                if s3: copy_probT(s, 1)
                if s2: low2(s)
                if s3: copy_probT(s, 3)
                if s1: residual1(s); stats1(s)
                if s0: head_norm(s)
                if s1: moments1(s)
                if s0: rotate(s)
                if ahead.works(4): divide(ahead)
                if s0: add_halves(s)
                if s1: normalize1(s)

            dve.wait_ge(zeros_set, 8)
            nc.vector.memset(xn[:, D:D + 1], 1.0)
            nc.vector.memset(xc[:, D:D + 1], 1.0)
            nc.vector.memset(ex[:, E:2 * E], -1.0)
            nc.vector.memset(top2[:, :], -1.0)
            for i in range(2):
                nc.vector.memset(v2[i][:, :, DH:DH + 1], 1.0)
            dve.wait_ge(consts_in, 16 * CONSTS)
            nc.vector.tensor_tensor(rope[:, :], rope_sb[:, :], g_sb[:, :], ALU.mult).then_inc(rope_set, 1)
            dve.wait_ge(rope_set, 1)
            dve.wait_ge(weights_in, 16 * WEIGHTS)
            run(dve, step)

        @block.gpsimd
        def _(pool):
            def rstd0_(s):
                pool.wait_ge(var0_set, s.upto(0))
                if s.began(0, 1):
                    pool.wait_ge(xn_set, s.upto(0, 1))
                nc.gpsimd.tensor_tensor(rstd0[:, :], var0[:, :], minus_half[:, 0:1], ALU.pow)\
                    .then_inc(rstd0_set, 1)

            def rstd1_(s):
                pool.wait_ge(var1_set, s.upto(1))
                if s.began(1, 1):
                    pool.wait_ge(xc_set, s.upto(1, 1))
                nc.gpsimd.tensor_tensor(rstd1[:, :], var1[:, :], minus_half[:, 0:1], ALU.pow)\
                    .then_inc(rstd1_set, 1)

            def square_qk(s):
                pool.wait_ge(qk1_copied, s.upto(0))
                if s.began(0, 1):
                    pool.wait_ge(ss_set, s.upto(0, 1))
                q = qk1[s.par(0)][:, :, :]
                nc.gpsimd.tensor_tensor(sq[:, :, :], q, q, ALU.mult).then_inc(sq_set, 1)

            def rms_(s):
                pool.wait_ge(ms_set, s.upto(0))
                if s.began(0, 1):
                    pool.wait_ge(qkn_set, s.upto(0, 1))
                nc.gpsimd.tensor_tensor(rms[:, :], ms[:, :], minus_half[:, :], ALU.pow)\
                    .then_inc(rms_set, 1)

            def own_half(s):
                pool.wait_ge(qkn_set, s.upto(0))
                if s.began(0, 1):
                    pool.wait_ge(qkr_set, s.upto(0, 1))
                nc.gpsimd.tensor_tensor(own[:, :, :], qkn[:, :, :],
                                        rope[:, 0:DH].unsqueeze(1).broadcast_to([T, 2 * H, DH]),
                                        ALU.mult).then_inc(own_set, 1)

            def mask(s, g):
                pool.wait_ge(square_set[g], s.upto(1))
                heads = pat[:, g * HR:(g + 1) * HR, :]
                nc.gpsimd.tensor_tensor(heads, heads, keep[:, :].unsqueeze(1).broadcast_to([T, HR, T]),
                                        ALU.mult).then_inc(pat_set[g], 1)

            def add_bias(s):
                pool.wait_ge(h1_set, s.upto(2))
                if s.began(2, 2):
                    pool.wait_ge(out_set, s.upto(2, 2))
                nc.gpsimd.tensor_tensor(h1b[s.par(2)][:, :], h1[s.par(2)][:, :], proj_b[:, :], ALU.add)\
                    .then_inc(h1b_set, 1)

            def step(s):
                s0, s1, s2, _, _ = (s.works(k) for k in range(STAGES))
                if s0: rstd0_(s)
                if s1: mask(s, 1); mask(s, 0); mask(s, 2)
                if s0: square_qk(s); rms_(s); own_half(s)
                if s1: rstd1_(s)
                if s2: add_bias(s)

            for z in v1 + v2:
                nc.gpsimd.memset(z[:, :, :], 0.0).then_inc(zeros_set, 1)
            for z in (xn, xc):
                nc.gpsimd.memset(z[:, :], 0.0).then_inc(zeros_set, 1)
            nc.gpsimd.memset(slot1[:, :, :].bitcast(fp32), 0.0).then_inc(zeros_set, 1)
            nc.gpsimd.memset(minus_half[:, :], -0.5).then_inc(zeros_set, 1)
            pool.wait_ge(zeros_set, 8)
            pool.wait_ge(rope_set, 1)
            pool.wait_ge(weights_in, 16 * WEIGHTS)
            run(pool, step)


def kernel(**inputs):
    import numpy as np
    import concourse.bacc as bacc
    from concourse.bass_utils import run_bass_kernel_spmd

    IMG, C, SIDE, PATCH, PER_TILE = 64, 3, 96, 16, 3
    H, DH, D, BASE = 12, 16, 192, 512.0
    N = SIDE // PATCH
    S = N * N
    TILES = -(-IMG // PER_TILE)
    T = PER_TILE * S

    x = np.asarray(inputs["x"])
    starts = [min(PER_TILE * t, IMG - PER_TILE) for t in range(TILES)]
    xt = x.reshape(IMG, C, N, PATCH, N, PATCH).transpose(1, 3, 5, 0, 2, 4).reshape(-1, 128, IMG, S)
    x_tiles = np.stack([xt[:, :, a:a + PER_TILE] for a in starts])
    x_tiles = x_tiles.transpose(0, 2, 1, 3, 4).reshape(TILES, 128, -1, T)

    g = {n: np.asarray(a) for n, a in inputs.items() if n != "x"}

    def strips(a):
        return a.reshape(2, 2, 3, DH, -1).transpose(0, 2, 1, 3, 4).reshape(a.shape)

    for c in "qk":
        for n in ("L0_attn_W", "L0_attn_b"):
            g[n + c] = strips(g[n + c])

    def strips_qkv(a):
        return np.concatenate([strips(a[:D]), strips(a[D:2 * D]), a[2 * D:]], 0)

    g["L0_ffn_Wqkv"] = strips_qkv(g["L0_ffn_Wqkv"])
    g["L0_ffn_bqkv"] = strips_qkv(g["L0_ffn_bqkv"])
    g["L0_ffn_bb"] = np.stack([strips_qkv(a) for a in g["L0_ffn_bb"]])
    g["L0_ffn_Bm"] = np.stack([strips_qkv(a) for a in g["L0_ffn_Bm"]])
    row = lambda n: g[n].reshape(1, -1)
    w_tok = g["L0_tok_W"].T.reshape(-1, 128, D).transpose(1, 0, 2)
    w_qkv1 = np.concatenate([np.concatenate([g["L0_attn_W" + c].T for c in "qkv"], 1),
                             np.concatenate([row("L0_attn_b" + c) for c in "qkv"], 1)], 0)
    a = g["L0_ffn_A"].reshape(-1, D)
    w_gate = np.concatenate([np.concatenate([a.T, g["L0_ffn_Wg"].T], 1),
                             np.concatenate([row("L0_ffn_ba"), row("L0_ffn_bg")], 1)], 0)
    w_qkv2 = np.concatenate([g["L0_ffn_Wqkv"].T, row("L0_ffn_bqkv"), g["L0_ffn_bb"]], 0)
    w_lora = g["L0_ffn_Bm"].transpose(0, 2, 1).reshape(-1, 3 * D)
    w_o1 = np.zeros((4, 32, H // 4, D), np.float32)
    w_o1[:, 0:DH] = g["L0_attn_Wo"].T.reshape(H // 4, 4, DH, D).transpose(1, 2, 0, 3)
    gain = g["L0_attn_g"]
    g_rows = np.concatenate([gain, gain[DH // 2:], gain[:DH // 2]]).reshape(1, -1)

    inv = (1.0 / BASE ** (np.arange(0, DH, 2, dtype=np.float32) / DH)).astype(np.float32)
    at = np.arange(T)
    freqs = np.outer((at % S).astype(np.float32), inv).astype(np.float32)
    cos, sin = np.cos(freqs), np.sin(freqs)
    rope_rows = np.concatenate([cos, cos, sin, -sin], 1).astype(np.float32)
    same = (at[:, None] // S) == (at[None, :] // S)
    causal_keep = (same & (at[:, None] <= at[None, :])).astype(np.float32)
    image = (at[:, None] // S == np.arange(PER_TILE)[None, :]).astype(np.float32)
    image_rows = np.zeros((T, 2, H, 64 - 3 * DH), np.float32)
    image_rows[:, 0, :, 0:PER_TILE] = image[:, None, :]
    image_rows[:, 1, :, 0:PER_TILE] = (1.0 - image[:, None, :]) * np.float32(-2.0 ** 99)
    identity = np.eye(128, dtype=np.float32)

    nc = bacc.Bacc("TRN2", target_bir_lowering=False, num_devices=1)
    arrays = dict(x_tiles=x_tiles, w_tok=w_tok, b_tok=row("L0_tok_b"), w_qkv1=w_qkv1,
                  w_o1=w_o1.reshape(128, H // 4, D), g_rows=g_rows, rope_rows=rope_rows,
                  causal_keep=causal_keep, w_gate=w_gate, w_qkv2=w_qkv2, w_lora=w_lora,
                  w_proj=g["L0_ffn_Wproj"].T, b_proj=row("L0_ffn_bproj"),
                  image_rows=image_rows, identity=identity)
    arrays = {n: np.ascontiguousarray(v) for n, v in arrays.items()}
    args = {n: nc.dram_tensor("in_" + n, v.shape, mybir.dt.from_np(v.dtype), kind="ExternalInput").ap()
            for n, v in arrays.items()}
    args["out"] = nc.dram_tensor("out_h", (TILES, T, D), mybir.dt.float32, kind="ExternalOutput").ap()
    vit_tower(nc, **args)
    r = run_bass_kernel_spmd(nc, [{"in_" + n: v for n, v in arrays.items()}], core_ids=[0])
    h = r.results[0]["out_h"].reshape(TILES, PER_TILE, S, D)
    own = PER_TILE * (TILES - 1) - starts[-1]
    return np.concatenate([h[:-1].reshape(-1, S, D), h[-1, own:]], 0)
```

```python
import concourse.bass as bass
from concourse import mybir
from contextlib import ExitStack


def vit_tower(nc, x_tiles, w_tok, b_tok, w_qkv1, w_o1, g_rows, rope_rows, causal_keep,
              w_gate, w_qkv2, w_lora, w_proj, b_proj, image_rows, identity, out):
    fp32 = mybir.dt.float32
    fp32r = mybir.dt.float32r
    ALU = mybir.AluOpType
    ACT = mybir.ActivationFunctionType
    AX = mybir.AxisListType

    TILES, P, CK, T = x_tiles.shape
    D = w_tok.shape[2]
    H = 12
    DH = D // H
    HALF = DH // 2
    D2 = D - P
    SLOT = 64
    PAIR = P // SLOT
    GROUPS = H // PAIR
    GR = 2
    HR = GR * PAIR
    ROUNDS = H // HR
    VSLOT = 32
    VSTRIPS = P // VSLOT
    VGROUPS = H // VSTRIPS
    E = 8
    R = w_lora.shape[0]
    RANK = R // E
    SPLIT = 3 * DH
    KX = SPLIT + 3
    LN_EPS = 1e-5
    RMS_EPS = 1e-6
    LORA_SCALE = 2.0
    SM_SCALE = DH ** -0.5
    STAGES = 5

    with ExitStack() as ctx:
        def sb(name, shape, dtype=fp32):
            return ctx.enter_context(nc.sbuf_tensor(name, shape, dtype))

        def bank(name):
            return ctx.enter_context(nc.psum_tensor(name, [P, 512], fp32))

        def sem(name):
            return ctx.enter_context(nc.semaphore(name))

        tok_w = sb("tok_w", [P, CK, D])
        tok_b = sb("tok_b", [T, D])
        qkv1_w0 = sb("qkv1_w0", [P, 3 * D])
        qkv1_w1 = sb("qkv1_w1", [D2 + 1, 3 * D])
        o1_w = sb("o1_w", [P, VGROUPS, D])
        gate_w0 = sb("gate_w0", [P, R + E])
        gate_w1 = sb("gate_w1", [D2 + 1, R + E])
        qkv2_w0 = sb("qkv2_w0", [P, 3 * D])
        qkv2_w1 = sb("qkv2_w1", [D2 + 1 + E, 3 * D])
        lora_w = sb("lora_w", [R, 3 * D])
        proj_w0 = sb("proj_w0", [P, D])
        proj_w1 = sb("proj_w1", [D2, D])
        proj_b = sb("proj_b", [T, D])
        ident = sb("ident", [P, P])
        keep = sb("keep", [T, T])
        g_sb = sb("g_sb", [T, 2 * DH])
        rope_sb = sb("rope_sb", [T, 2 * DH])
        rope = sb("rope", [T, 2 * DH])
        warm = sb("warm", [T, 1])
        minus_half = sb("minus_half", [T, 2 * H])

        x_sb = [sb(f"x_sb{i}", [P, CK, T]) for i in range(2)]
        out_sb = [sb(f"out_sb{i}", [T, D]) for i in range(2)]
        h0 = [sb(f"h0_{i}", [T, D]) for i in range(2)]
        qk1 = [sb(f"qk1_{i}", [T, 2 * H, DH]) for i in range(2)]
        v1 = [sb(f"v1_{i}", [T, H, VSLOT]) for i in range(2)]
        h1 = [sb(f"h1_{i}", [T, D]) for i in range(2)]
        h1b = [sb(f"h1b_{i}", [T, D]) for i in range(2)]
        v2 = [sb(f"v2_{i}", [T, H, VSLOT]) for i in range(2)]

        stat0 = sb("stat0", [T, 6])
        mv0 = sb("mv0", [T, 2])
        var0 = sb("var0", [T, 1])
        rstd0 = sb("rstd0", [T, 1])
        xn = sb("xn", [T, 2 * P])
        xnT = sb("xnT", [P, 2, T])
        sq = sb("sq", [T, 2 * H, DH])
        ss = sb("ss", [T, 2 * H])
        ms = sb("ms", [T, 2 * H])
        rms = sb("rms", [T, 2 * H])
        qkn = sb("qkn", [T, 2 * H, DH])
        own = sb("own", [T, 2 * H, DH])
        other = sb("other", [T, 2 * H, DH])
        qkr = sb("qkr", [T, 2 * H, DH])
        slot1 = sb("slot1", [T, 2 * H, SLOT], fp32r)
        k1T = sb("k1T", [P, GROUPS, T], fp32r)
        q1T = sb("q1T", [P, GROUPS, PAIR, T], fp32r)
        pat = sb("pat", [T, H, T])
        z1T = sb("z1T", [P, VGROUPS, T])
        stat1 = sb("stat1", [T, 6])
        mv1 = sb("mv1", [T, 2])
        var1 = sb("var1", [T, 1])
        rstd1 = sb("rstd1", [T, 1])
        xc = sb("xc", [T, 2 * P])
        x2T = sb("x2T", [P, 2, T])
        nmax = sb("nmax", [T, 1])
        ex = sb("ex", [T, 2 * E])
        exsum = sb("exsum", [T, 1])
        rsum = sb("rsum", [T, 1])
        lora_scale = sb("lora_scale", [T, 1])
        top = sb("top", [T, E])
        top2 = sb("top2", [T, E])
        rest = sb("rest", [T, 2 * E])
        picked = sb("picked", [T, E])
        hw = sb("hw", [T, E, RANK])
        catT = sb("catT", [P, 2, T])
        slot2 = sb("slot2", [T, 2 * H, SLOT], fp32r)
        q2T = sb("q2T", [P, GROUPS, T], fp32r)
        k2T = sb("k2T", [P, GROUPS, PAIR, T], fp32r)
        smax = sb("smax", [T, H])
        prob = sb("prob", [T, H, T])
        probT = sb("probT", [T, H, T])
        zsT = sb("zsT", [P, VGROUPS, T])
        rden = sb("rden", [T, H])
        z2 = sb("z2", [T, H, DH])
        z2T = sb("z2T", [P, 2, T])

        banks = [bank(f"bank{i}") for i in range(8)]

        ps_zs = banks[0][0:T, 0:H * VSLOT]
        ps_z2T = banks[0][:, 0:2 * T]
        ps_y2 = banks[0][0:T, 0:D]
        ps_tok = banks[0][0:T, 0:D]
        ps_xnT = banks[0][:, D:D + 2 * T]
        ps_qk1 = banks[2][0:T, 0:2 * D]
        ps_gate = banks[2][0:T, 0:R + E]
        ps_qk2 = banks[2][0:T, 0:2 * D]
        ps_v1 = banks[1][0:T, 0:D]
        ps_x2T = banks[1][:, D:D + 2 * T]
        ps_v2 = banks[7][0:T, 0:D]
        ps_slot1T = [banks[b][:, 0:2 * GR * T] for b in (3, 4, 3)]
        ps_s1 = [banks[b][0:T, 0:HR * T] for b in (4, 3, 4)]
        ps_z1T = banks[3][:, 0:VGROUPS * T]
        ps_y1 = banks[4][0:T, 0:D]
        ps_slot2T = [banks[b][:, 0:2 * GR * T] for b in (5, 6, 5)]
        ps_s2 = [banks[b][0:T, 0:HR * T] for b in (6, 5, 6)]
        ps_pT = [banks[b][0:T, 0:HR * T] for b in (7, 5, 6)]
        ps_zsT = banks[5][:, 0:VGROUPS * T]

        tok_in = sem("tok_in")
        tok_end_in = sem("tok_end_in")
        ident_in = sem("ident_in")
        qkv1_in = sem("qkv1_in")
        weights_in = sem("weights_in")
        consts_in = sem("consts_in")
        slots_in = sem("slots_in")
        zeros_set = sem("zeros_set")
        fills_set = sem("fills_set")
        rope_set = sem("rope_set")
        x_in = [sem(f"x_in{i}") for i in range(2)]
        out_stored = sem("out_stored")
        tok_done = sem("tok_done")
        h0_set = sem("h0_set")
        stat0_set = sem("stat0_set")
        mv0_set = sem("mv0_set")
        var0_set = sem("var0_set")
        rstd0_set = sem("rstd0_set")
        xn_set = sem("xn_set")
        xnT_done = sem("xnT_done")
        xnT_copied = sem("xnT_copied")
        qk1_done = sem("qk1_done")
        v1_done = sem("v1_done")
        qk1_copied = sem("qk1_copied")
        v1_copied = sem("v1_copied")
        sq_set = sem("sq_set")
        ss_set = sem("ss_set")
        ms_set = sem("ms_set")
        rms_set = sem("rms_set")
        qkn_set = sem("qkn_set")
        own_set = sem("own_set")
        other_set = sem("other_set")
        qkr_set = sem("qkr_set")
        high1_set = sem("high1_set")
        slot1_set = sem("slot1_set")
        slot1T_done = [sem(f"slot1T_done{i}") for i in range(ROUNDS)]
        slot1T_copied = [sem(f"slot1T_copied{i}") for i in range(ROUNDS)]
        s1_done = [sem(f"s1_done{i}") for i in range(ROUNDS)]
        square_set = [sem(f"square_set{i}") for i in range(ROUNDS)]
        pat_set = [sem(f"pat_set{i}") for i in range(ROUNDS)]
        z1T_done = sem("z1T_done")
        z1T_copied = sem("z1T_copied")
        y1_done = sem("y1_done")
        h1_set = sem("h1_set")
        h1b_set = sem("h1b_set")
        stat1_set = sem("stat1_set")
        mv1_set = sem("mv1_set")
        var1_set = sem("var1_set")
        rstd1_set = sem("rstd1_set")
        xc_set = sem("xc_set")
        x2T_done = sem("x2T_done")
        x2T_copied = sem("x2T_copied")
        gate_done = sem("gate_done")
        nmax_set = sem("nmax_set")
        ex_set = sem("ex_set")
        rsum_set = sem("rsum_set")
        scale_set = sem("scale_set")
        top_set = sem("top_set")
        top2_set = sem("top2_set")
        rest_set = sem("rest_set")
        picked_set = sem("picked_set")
        combine_set = sem("combine_set")
        hw_set = sem("hw_set")
        catT_done = sem("catT_done")
        catT_copied = sem("catT_copied")
        qk2_done = sem("qk2_done")
        v2_done = sem("v2_done")
        high2_set = sem("high2_set")
        slot2_set = sem("slot2_set")
        v2_copied = sem("v2_copied")
        slot2T_done = [sem(f"slot2T_done{i}") for i in range(ROUNDS)]
        slot2T_copied = [sem(f"slot2T_copied{i}") for i in range(ROUNDS)]
        s2_done = [sem(f"s2_done{i}") for i in range(ROUNDS)]
        smax_set = [sem(f"smax_set{i}") for i in range(ROUNDS)]
        shift_set = [sem(f"shift_set{i}") for i in range(ROUNDS)]
        prob_set = [sem(f"prob_set{i}") for i in range(ROUNDS)]
        pT_done = [sem(f"pT_done{i}") for i in range(ROUNDS)]
        pT_copied = [sem(f"pT_copied{i}") for i in range(ROUNDS)]
        zsT_done = sem("zsT_done")
        zsT_copied = sem("zsT_copied")
        zs_done = sem("zs_done")
        rden_set = sem("rden_set")
        z2_set = sem("z2_set")
        z2T_done = sem("z2T_done")
        z2T_copied = sem("z2T_copied")
        y2_done = sem("y2_done")
        out_set = sem("out_set")

        WEIGHTS = 9
        CONSTS = 3

        class Step:

            def __init__(self, eng, n, parity):
                self.eng, self.n, self.parity = eng, n, parity
                self.fixed = isinstance(n, int)

            def other(self, by):
                return Step(self.eng, self.n + by, (self.parity + by) % 2)

            def works(self, stage):
                return not self.fixed or 0 <= self.n - stage < TILES

            def par(self, stage):
                return (self.parity + stage) % 2

            def began(self, stage, back=0):
                return not self.fixed or self.n - stage - back >= 0

            def upto(self, stage, back=0):
                count = self.n - stage + (1 - back)
                return min(count, TILES) if self.fixed else count

            def patches(self):
                return self.n * 8 + (16 - 8 * self.parity)

        FIRST = 6
        STEPS = TILES + STAGES - 1

        def run(eng, step):
            for n in range(-1, FIRST):
                step(Step(eng, n, n % 2))
            with eng.Fori(FIRST, TILES, 2) as n:
                step(Step(eng, n, 0))
                step(Step(eng, n + 1, 1))
            for n in range(TILES, STEPS + 1):
                step(Step(eng, n, n % 2))

        block = ctx.enter_context(nc.Block())

        @block.sync
        def _(sp):
            sp.dma_start(tok_w[:, 0:CK // 2, :], w_tok[:, 0:CK // 2]).then_inc(tok_in, 16)
            sp.dma_start(tok_w[:, CK // 2:CK, :], w_tok[:, CK // 2:CK]).then_inc(tok_end_in, 16)
            for dst, src in ((qkv1_w0, w_qkv1[0:P]), (qkv1_w1, w_qkv1[P:D + 1])):
                sp.dma_start(dst[:, :], src).then_inc(qkv1_in, 16)
            sp.dma_start(x_sb[1][:, :, :], x_tiles[1]).then_inc(x_in[1], 16)
            sp.dma_start(o1_w[:, :, :], w_o1).then_inc(weights_in, 16)
            for dst, src in ((gate_w0, w_gate[0:P]),
                             (gate_w1, w_gate[P:D + 1]), (qkv2_w0, w_qkv2[0:P]),
                             (qkv2_w1, w_qkv2[P:D + 1 + E]), (lora_w, w_lora),
                             (proj_w0, w_proj[0:P]), (proj_w1, w_proj[P:D]),
                             (proj_b, b_proj.broadcast_to([T, D]))):
                sp.dma_start(dst[:, :], src).then_inc(weights_in, 16)

            x_pairs = x_tiles.rearrange("(m k) p c t -> m k p c t", k=2)
            out_pairs = out.rearrange("(m k) t d -> m k t d", k=2)

            def load(m, k):
                sp.wait_ge(tok_done, 2 * m + (k - 1))
                sp.dma_start(x_sb[k][:, :, :], x_pairs[m, k]).then_inc(x_in[k], 16)

            def store(m, k):
                sp.wait_ge(out_set, 2 * m + (k + 1))
                sp.dma_start(out_pairs[m, k], out_sb[k][:, :]).then_inc(out_stored, 16)

            for n in range(2, FIRST):
                load(n // 2, n % 2)
            with sp.Fori(FIRST // 2, TILES // 2) as m:
                for k in range(2):
                    load(m, k)
                    store(m - FIRST // 2, k)
            for t in range(TILES - FIRST, TILES):
                store(t // 2, t % 2)
            sp.wait_ge(out_stored, 16 * TILES)

        @block.tensor
        def _(pe):
            def transpose(dst, src):
                n = src.shape[0]
                return nc.tensor.transpose(dst, src, ident[0:n, 0:n])

            def tokens(s):
                if not s.began(0, 1):
                    pe.wait_ge(tok_in, 16)
                pe.wait_ge(x_in[s.parity], s.patches())
                if s.began(0, 1):
                    pe.wait_ge(xnT_copied, s.upto(0, 1))
                if s.began(4):
                    pe.wait_ge(z2_set, s.upto(4))
                for c in range(CK // 2):
                    nc.tensor.matmul(ps_tok, x_sb[s.par(0)][:, c, :], tok_w[:, c, :],
                                     start=(c == 0), stop=False)

            def tokens_end(s):
                if not s.began(0, 1):
                    pe.wait_ge(tok_end_in, 16 * 2)
                for c in range(CK // 2, CK):
                    mm = nc.tensor.matmul(ps_tok, x_sb[s.par(0)][:, c, :], tok_w[:, c, :],
                                          start=False, stop=(c == CK - 1))
                mm.then_inc(tok_done, 1)

            def turn_xn(s):
                if not s.began(0, 1):
                    pe.wait_ge(ident_in, 16 * 2)
                pe.wait_ge(xn_set, s.upto(0))
                if s.began(4):
                    pe.wait_ge(out_set, s.upto(4))
                for c in range(2):
                    mm = transpose(ps_xnT[:, c * T:(c + 1) * T], xn[:, c * P:(c + 1) * P])
                mm.then_inc(xnT_done, 1)

            def project_qk1(s):
                if not s.began(0, 1):
                    pe.wait_ge(qkv1_in, 16 * 2)
                pe.wait_ge(xnT_copied, s.upto(0))
                if s.began(2, 1):
                    pe.wait_ge(slot2_set, s.upto(2, 1))
                if s.began(2):
                    pe.wait_ge(hw_set, s.upto(2))
                c = slice(0, 2 * D)
                nc.tensor.matmul(ps_qk1, xnT[:, 0, :], qkv1_w0[:, c], start=True, stop=False)
                nc.tensor.matmul(ps_qk1, xnT[0:D2 + 1, 1, :], qkv1_w1[:, c],
                                 start=False, stop=True).then_inc(qk1_done, 1)

            def project_v1(s):
                if not s.began(0, 1):
                    pe.wait_ge(qkv1_in, 16 * 2)
                pe.wait_ge(xnT_copied, s.upto(0))
                if s.began(2):
                    pe.wait_ge(x2T_copied, s.upto(2))
                c = slice(2 * D, 3 * D)
                nc.tensor.matmul(ps_v1, xnT[:, 0, :], qkv1_w0[:, c], start=True, stop=False)
                nc.tensor.matmul(ps_v1, xnT[0:D2 + 1, 1, :], qkv1_w1[:, c],
                                 start=False, stop=True).then_inc(v1_done, 1)

            def turn_slot1(s, i):
                if i < 2:
                    pe.wait_ge(slot1_set, s.upto(1))
                if i == 0 and s.began(1, 1):
                    pe.wait_ge(z1T_copied, s.upto(1, 1))
                if i == 1 and s.began(1, 1):
                    pe.wait_ge(h1_set, s.upto(1, 1))
                if i == 2:
                    pe.wait_ge(slot1T_copied[0], s.upto(1))
                for part in range(2):
                    for g in range(GR):
                        p = part * H + PAIR * (i * GR + g)
                        src = slot1[:, p:p + PAIR, :].bitcast(fp32).rearrange("t h d -> t (h d)")
                        c = (part * GR + g) * T
                        mm = transpose(ps_slot1T[i][:, c:c + T], src)
                mm.then_inc(slot1T_done[i], 1)

            def scores1(s, i):
                pe.wait_ge(slot1T_copied[i], s.upto(1))
                if i == 0:
                    pe.wait_ge(slot1T_copied[1], s.upto(1))
                elif i == 1:
                    pe.wait_ge(slot1T_copied[2], s.upto(1))
                else:
                    pe.wait_ge(square_set[0], s.upto(1))
                for g in range(GR):
                    mm = nc.tensor.matmul(ps_s1[i][:, g * PAIR * T:(g + 1) * PAIR * T],
                                          k1T[:, i * GR + g, :],
                                          q1T[:, i * GR + g, :, :].rearrange("p h t -> p (h t)"),
                                          start=True, stop=True)
                mm.then_inc(s1_done[i], 1)

            def values1(s):
                pe.wait_ge(square_set[1], s.upto(1))
                for i in range(ROUNDS):
                    pe.wait_ge(pat_set[i], s.upto(1))
                    for h in range(i * HR, (i + 1) * HR):
                        g, j = h // VSTRIPS, h % VSTRIPS
                        mm = nc.tensor.matmul(ps_z1T[j * VSLOT:(j + 1) * VSLOT, g * T:(g + 1) * T],
                                              v1[s.par(1)][:, h, :], pat[:, h, :],
                                              start=True, stop=True)
                mm.then_inc(z1T_done, 1)

            def output1(s):
                if not s.began(1, 1):
                    pe.wait_ge(weights_in, 16 * WEIGHTS)
                pe.wait_ge(z1T_copied, s.upto(1))
                pe.wait_ge(square_set[2], s.upto(1))
                for g in range(VGROUPS):
                    mm = nc.tensor.matmul(ps_y1, z1T[:, g, :], o1_w[:, g, :],
                                          start=(g == 0), stop=(g == VGROUPS - 1))
                mm.then_inc(y1_done, 1)

            def turn_x2(s):
                pe.wait_ge(xc_set, s.upto(2))
                if s.began(2, 1):
                    pe.wait_ge(catT_copied, s.upto(2, 1))
                pe.wait_ge(v1_copied, s.upto(1))
                for c in range(2):
                    mm = transpose(ps_x2T[:, c * T:(c + 1) * T], xc[:, c * P:(c + 1) * P])
                mm.then_inc(x2T_done, 1)

            def gate(s):
                if not s.began(2, 1):
                    pe.wait_ge(weights_in, 16 * WEIGHTS)
                pe.wait_ge(x2T_copied, s.upto(2))
                if s.began(2, 1):
                    pe.wait_ge(slot2_set, s.upto(2, 1))
                pe.wait_ge(qk1_copied, s.upto(1))
                nc.tensor.matmul(ps_gate, x2T[:, 0, :], gate_w0[:, :], start=True, stop=False)
                nc.tensor.matmul(ps_gate, x2T[0:D2 + 1, 1, :], gate_w1[:, :],
                                 start=False, stop=True).then_inc(gate_done, 1)

            def turn_cat(s):
                pe.wait_ge(combine_set, s.upto(2))
                pe.wait_ge(hw_set, s.upto(2))
                pe.wait_ge(v1_copied, s.upto(0))
                transpose(ps_x2T[:, 0:T], xc[:, P:2 * P])
                transpose(ps_x2T[:, T:2 * T], hw[:, :, :].rearrange("t e r -> t (e r)"))\
                    .then_inc(catT_done, 1)

            def project_qk2(s):
                pe.wait_ge(catT_copied, s.upto(2))
                pe.wait_ge(qk1_copied, s.upto(0))
                c = slice(0, 2 * D)
                nc.tensor.matmul(ps_qk2, x2T[:, 0, :], qkv2_w0[:, c], start=True, stop=False)
                nc.tensor.matmul(ps_qk2, catT[0:D2 + 1 + E, 0, :], qkv2_w1[:, c],
                                 start=False, stop=False)
                nc.tensor.matmul(ps_qk2, catT[:, 1, :], lora_w[:, c],
                                 start=False, stop=True).then_inc(qk2_done, 1)

            def project_v2(s):
                pe.wait_ge(catT_copied, s.upto(2))
                if s.began(3):
                    pe.wait_ge(pT_copied[0], s.upto(3))
                c = slice(2 * D, 3 * D)
                nc.tensor.matmul(ps_v2, x2T[:, 0, :], qkv2_w0[:, c], start=True, stop=False)
                nc.tensor.matmul(ps_v2, catT[0:D2 + 1 + E, 0, :], qkv2_w1[:, c],
                                 start=False, stop=False)
                nc.tensor.matmul(ps_v2, catT[:, 1, :], lora_w[:, c],
                                 start=False, stop=True).then_inc(v2_done, 1)

            def turn_slot2(s, i):
                if i < 2:
                    pe.wait_ge(slot2_set, s.upto(3))
                if i == 0 and s.began(3, 1):
                    pe.wait_ge(zsT_copied, s.upto(3, 1))
                if i == 1 and s.began(3, 1):
                    pe.wait_ge(pT_copied[2], s.upto(3, 1))
                if i == 2:
                    pe.wait_ge(slot2T_copied[0], s.upto(3))
                for part in range(2):
                    for g in range(GR):
                        p = part * H + PAIR * (i * GR + g)
                        src = slot2[:, p:p + PAIR, :].bitcast(fp32).rearrange("t h d -> t (h d)")
                        c = (part * GR + g) * T
                        mm = transpose(ps_slot2T[i][:, c:c + T], src)
                mm.then_inc(slot2T_done[i], 1)

            def scores2(s, i):
                pe.wait_ge(slot2T_copied[i], s.upto(3))
                if i == 0:
                    pe.wait_ge(slot2T_copied[1], s.upto(3))
                elif i == 1:
                    pe.wait_ge(slot2T_copied[2], s.upto(3))
                else:
                    pe.wait_ge(shift_set[0], s.upto(3))
                for g in range(GR):
                    mm = nc.tensor.matmul(ps_s2[i][:, g * PAIR * T:(g + 1) * PAIR * T],
                                          q2T[:, i * GR + g, :],
                                          k2T[:, i * GR + g, :, :].rearrange("p h t -> p (h t)"),
                                          start=True, stop=True)
                mm.then_inc(s2_done[i], 1)

            def turn_prob(s, i):
                pe.wait_ge(prob_set[i], s.upto(3))
                if i == 0:
                    pe.wait_ge(v2_copied, s.upto(3))
                for g in range(HR):
                    mm = transpose(ps_pT[i][:, g * T:(g + 1) * T], prob[:, i * HR + g, :])
                mm.then_inc(pT_done[i], 1)

            def values2(s):
                pe.wait_ge(pT_copied[1], s.upto(3))
                for i in range(ROUNDS):
                    pe.wait_ge(pT_copied[i], s.upto(3))
                    for h in range(i * HR, (i + 1) * HR):
                        g, j = h // VSTRIPS, h % VSTRIPS
                        mm = nc.tensor.matmul(ps_zsT[j * VSLOT:(j + 1) * VSLOT, g * T:(g + 1) * T],
                                              v2[s.par(3)][:, h, :], probT[:, h, :],
                                              start=True, stop=True)
                mm.then_inc(zsT_done, 1)

            def turn_zs(s):
                pe.wait_ge(zsT_copied, s.upto(4))
                pe.wait_ge(xnT_copied, s.upto(0, 1))
                for g in range(VGROUPS):
                    mm = transpose(ps_zs[:, g * P:(g + 1) * P], zsT[:, g, :])
                mm.then_inc(zs_done, 1)

            def turn_z2(s):
                pe.wait_ge(z2_set, s.upto(4))
                pe.wait_ge(h0_set, s.upto(0))
                z = z2[:, :, :].rearrange("t h d -> t (h d)")
                transpose(ps_z2T[:, 0:T], z[:, 0:P])
                transpose(ps_z2T[0:D2, T:2 * T], z[:, P:D]).then_inc(z2T_done, 1)

            def output2(s):
                pe.wait_ge(z2T_copied, s.upto(4))
                nc.tensor.matmul(ps_y2, z2T[:, 0, :], proj_w0[:, :], start=True, stop=False)
                nc.tensor.matmul(ps_y2, z2T[0:D2, 1, :], proj_w1[:, :],
                                 start=False, stop=True).then_inc(y2_done, 1)

            def step(s):
                s0, s1, s2, s3, s4 = (s.works(k) for k in range(STAGES))
                ahead = s.other(1)
                behind = s.other(-1)
                if s3: turn_slot2(s, 1); turn_slot2(s, 0)
                if s0: tokens(s); tokens_end(s)
                if behind.works(2): project_v2(behind)
                if s4: turn_z2(s)
                if s2: turn_x2(s)
                if s3: scores2(s, 0); turn_slot2(s, 2)
                if s2: gate(s)
                if s1: turn_slot1(s, 0)
                if s4: output2(s)
                if s1: turn_slot1(s, 1)
                if s3: scores2(s, 1); scores2(s, 2)
                if s0: turn_xn(s)
                if s1: turn_slot1(s, 2); scores1(s, 0)
                if s0: project_v1(s); project_qk1(s)
                if s1: scores1(s, 2); scores1(s, 1)
                if s2: turn_cat(s)
                if s3: turn_prob(s, 0); turn_prob(s, 1)
                if s2: project_qk2(s)
                if s3: turn_prob(s, 2)
                if s1: values1(s)
                if s3: values2(s)
                if s1: output1(s)
                if ahead.works(4): turn_zs(ahead)

            run(pe, step)

        @block.scalar
        def _(act):
            copy = nc.scalar.copy

            def copy_xnT(s):
                act.wait_ge(xnT_done, s.upto(0))
                copy(xnT[:, :, :], ps_xnT.rearrange("p (c t) -> p c t", c=2)).then_inc(xnT_copied, 1)

            def copy_qk1(s):
                act.wait_ge(qk1_done, s.upto(0))
                if s.began(0, 2):
                    act.wait_ge(qkn_set, s.upto(0, 2))
                copy(qk1[s.par(0)][:, :, :].rearrange("t h d -> t (h d)"), ps_qk1).then_inc(qk1_copied, 1)

            def copy_v1(s):
                act.wait_ge(v1_done, s.upto(0))
                if s.began(0, 2):
                    act.wait_ge(z1T_done, s.upto(0, 2))
                copy(v1[s.par(0)][:, :, 0:DH], ps_v1.rearrange("t (h d) -> t h d", d=DH)).then_inc(v1_copied, 1)

            def high_parts(slot, src, out_sem):
                q, k = slot[:, 0:H, :], slot[:, H:2 * H, :]
                for dst, part in ((q[:, :, 0:DH], 0), (q[:, :, 2 * DH:3 * DH], 0),
                                  (k[:, :, 0:DH], 1), (k[:, :, DH:2 * DH], 1)):
                    op = copy(dst, src[:, part * H:(part + 1) * H, :])
                op.then_inc(out_sem, 1)

            def high1(s):
                act.wait_ge(qkr_set, s.upto(0))
                if s.began(0, 1):
                    act.wait_ge(slot1T_done[1], s.upto(0, 1))
                    act.wait_ge(slot1T_done[2], s.upto(0, 1))
                high_parts(slot1, qkr[:, :, :], high1_set)

            def copy_slot1T(s, i):
                act.wait_ge(slot1T_done[i], s.upto(1))
                if s.began(1, 1):
                    act.wait_ge(s1_done[i], s.upto(1, 1))
                parts = ps_slot1T[i].rearrange("p (c g t) -> p c g t", c=2, g=GR)
                groups = slice(i * GR, (i + 1) * GR)
                copy(k1T[:, groups, :], parts[:, 1])
                for h in range(PAIR):
                    rows = slice(h * SLOT, (h + 1) * SLOT)
                    op = copy(q1T[rows, groups, h, :], parts[rows, 0])
                op.then_inc(slot1T_copied[i], 1)

            def squares(s, g):
                act.wait_ge(s1_done[g], s.upto(1))
                if g < 2:
                    if s.began(1, 1):
                        act.wait_ge(z1T_done, s.upto(1, 1))
                nc.scalar.activation(pat[:, g * HR:(g + 1) * HR, :],
                                     ps_s1[g].rearrange("t (h k) -> t h k", h=HR),
                                     ACT.Square, scale=1.0 / DH).then_inc(square_set[g], 1)

            def copy_x2T(s):
                act.wait_ge(x2T_done, s.upto(2))
                if s.began(2, 1):
                    act.wait_ge(qk2_done, s.upto(2, 1))
                if s.began(2, 1):
                    act.wait_ge(v2_done, s.upto(2, 1))
                copy(x2T[:, :, :], ps_x2T.rearrange("p (c t) -> p c t", c=2)).then_inc(x2T_copied, 1)

            def router_exp(s):
                act.wait_ge(nmax_set, s.upto(2))
                if s.began(2, 1):
                    act.wait_ge(picked_set, s.upto(2, 1))
                nc.scalar.activation(ex[:, 0:E], ps_gate[:, R:R + E], ACT.Exp, bias=nmax[:, 0:1],
                                     accum_out=exsum[:, 0:1]).then_inc(ex_set, 1)

            def copy_catT(s):
                act.wait_ge(catT_done, s.upto(2))
                copy(catT[:, :, :], ps_x2T.rearrange("p (c t) -> p c t", c=2)).then_inc(catT_copied, 1)

            def high2(s):
                act.wait_ge(qk2_done, s.upto(2))
                if s.began(3):
                    act.wait_ge(slot2T_done[1], s.upto(3))
                    act.wait_ge(slot2T_done[2], s.upto(3))
                high_parts(slot2, ps_qk2.rearrange("t (h d) -> t h d", d=DH), high2_set)

            def copy_v2(s):
                act.wait_ge(v2_done, s.upto(2))
                if s.began(2, 2):
                    act.wait_ge(zsT_done, s.upto(2, 2))
                copy(v2[s.par(2)][:, :, 0:DH], ps_v2.rearrange("t (h d) -> t h d", d=DH))\
                    .then_inc(v2_copied, 1)

            def copy_slot2T(s, i):
                act.wait_ge(slot2T_done[i], s.upto(3))
                if s.began(3, 1):
                    act.wait_ge(s2_done[i], s.upto(3, 1))
                parts = ps_slot2T[i].rearrange("p (c g t) -> p c g t", c=2, g=GR)
                groups = slice(i * GR, (i + 1) * GR)
                copy(q2T[:, groups, :], parts[:, 0])
                for h in range(PAIR):
                    rows = slice(h * SLOT, (h + 1) * SLOT)
                    op = copy(k2T[rows, groups, h, :], parts[rows, 1])
                op.then_inc(slot2T_copied[i], 1)

            def probs(s, g):
                act.wait_ge(shift_set[g], s.upto(3))
                heads = prob[:, g * HR:(g + 1) * HR, :]
                nc.scalar.activation(heads, heads, ACT.Exp, scale=SM_SCALE).then_inc(prob_set[g], 1)

            def copy_probT(s, g):
                act.wait_ge(pT_done[g], s.upto(3))
                if s.began(3, 1):
                    act.wait_ge(zsT_done, s.upto(3, 1))
                copy(probT[:, g * HR:(g + 1) * HR, :],
                     ps_pT[g].rearrange("t (h k) -> t h k", h=HR)).then_inc(pT_copied[g], 1)

            def copy_zsT(s):
                act.wait_ge(zsT_done, s.upto(3))
                if s.began(3, 1):
                    act.wait_ge(zs_done, s.upto(3, 1))
                copy(zsT[:, :, :], ps_zsT.rearrange("p (g t) -> p g t", g=VGROUPS)).then_inc(zsT_copied, 1)

            def copy_z2T(s):
                act.wait_ge(z2T_done, s.upto(4))
                copy(z2T[:, 0, :], ps_z2T[:, 0:T])
                copy(z2T[0:D2, 1, :], ps_z2T[0:D2, T:2 * T]).then_inc(z2T_copied, 1)

            def step(s):
                s0, s1, s2, s3, _ = (s.works(k) for k in range(STAGES))
                ahead = s.other(1)
                if s3: copy_slot2T(s, 2)
                if s1: copy_slot1T(s, 0)
                if s2: router_exp(s)
                if s1: copy_slot1T(s, 1)
                if s0: copy_xnT(s)
                if s1: copy_slot1T(s, 2); squares(s, 0)
                if s0: copy_v1(s)
                if s3: probs(s, 0); probs(s, 1)
                if s0: copy_qk1(s)
                if s2: copy_catT(s)
                if s1: squares(s, 2)
                if s3: probs(s, 2); copy_probT(s, 0)
                if s1: squares(s, 1)
                if s2: high2(s)
                if s3: copy_zsT(s)
                if ahead.works(3): copy_slot2T(ahead, 1); copy_slot2T(ahead, 0)
                if s0: high1(s)
                if ahead.works(2): copy_x2T(ahead)
                if ahead.works(4): copy_z2T(ahead)
                if s2: copy_v2(s)

            act.dma_start(x_sb[0][:, 0:CK // 2, :], x_tiles[0, :, 0:CK // 2]).then_inc(x_in[0], 16)
            act.dma_start(x_sb[0][:, CK // 2:CK, :], x_tiles[0, :, CK // 2:CK]).then_inc(tok_end_in, 16)
            act.dma_start(tok_b[:, :], b_tok.broadcast_to([T, D])).then_inc(ident_in, 16)
            act.dma_start(ident[:, :], identity).then_inc(ident_in, 16)
            act.dma_start(g_sb[:, :], g_rows.broadcast_to([T, 2 * DH])).then_inc(consts_in, 16)
            act.dma_start(rope_sb[:, :], rope_rows).then_inc(consts_in, 16)
            act.dma_start(keep[:, :], causal_keep).then_inc(consts_in, 16)
            for i in range(2):
                act.dma_start(slot2[:, i * H:(i + 1) * H, SPLIT:SLOT].bitcast(fp32), image_rows[:, i]).then_inc(slots_in, 16)
            act.wait_ge(zeros_set, 10)
            nc.scalar.activation(warm[:, :], minus_half[:, 0:1], ACT.Exp)
            act.wait_ge(slots_in, 16 * 2)
            run(act, step)

        @block.vector
        def _(dve):
            def embed(s):
                dve.wait_ge(tok_done, s.upto(0))
                if s.began(0, 2):
                    dve.wait_ge(h1_set, s.upto(0, 2))
                if s.began(0, 1):
                    dve.wait_ge(xn_set, s.upto(0, 1))
                nc.vector.tensor_tensor(h0[s.par(0)][:, :], ps_tok, tok_b[:, :], ALU.add).then_inc(h0_set, 1)

            def stats(s, stage, src, src_sem, stat, stat_sem):
                dve.wait_ge(src_sem, s.upto(stage))
                nc.vector.bn_stats(stat[:, :], src[:, :]).then_inc(stat_sem, 1)
                dve.wait_ge(stat_sem, s.upto(stage))

            def moments(mv, stat, mv_sem):
                nc.vector.bn_aggr(mv[:, :], stat[:, :]).then_inc(mv_sem, 1)

            def variance(s, stage, mv, mv_sem, var, var_sem):
                dve.wait_ge(mv_sem, s.upto(stage))
                nc.vector.tensor_scalar(var[:, :], mv[:, 1:2], LN_EPS, None, ALU.add).then_inc(var_sem, 1)

            def stats0(s):
                stats(s, 0, h0[s.par(0)], h0_set, stat0, stat0_set)

            def moments0(s):
                moments(mv0, stat0, mv0_set)
                variance(s, 0, mv0, mv0_set, var0, var0_set)

            def stats1(s):
                stats(s, 1, h1[s.par(1)], h1_set, stat1, stat1_set)

            def moments1(s):
                moments(mv1, stat1, mv1_set)
                variance(s, 1, mv1, mv1_set, var1, var1_set)

            def normalize0(s):
                dve.wait_ge(rstd0_set, s.upto(0))
                if s.began(0, 1):
                    dve.wait_ge(xnT_done, s.upto(0, 1))
                nc.vector.tensor_scalar(xn[:, 0:D], h0[s.par(0)][:, :], mv0[:, 0:1], rstd0[:, 0:1],
                                        ALU.subtract, ALU.mult).then_inc(xn_set, 1)

            def normalize1(s):
                dve.wait_ge(rstd1_set, s.upto(1))
                if s.began(1, 1):
                    dve.wait_ge(catT_done, s.upto(1, 1))
                nc.vector.tensor_scalar(xc[:, 0:D], h1[s.par(1)][:, :], mv1[:, 0:1], rstd1[:, 0:1],
                                        ALU.subtract, ALU.mult).then_inc(xc_set, 1)

            def head_sums(s):
                dve.wait_ge(sq_set, s.upto(0))
                nc.vector.tensor_reduce(ss[:, :], sq[:, :, :], AX.X, ALU.add).then_inc(ss_set, 1)
                dve.wait_ge(ss_set, s.upto(0))
                nc.vector.tensor_scalar(ms[:, :], ss[:, :], 1.0 / DH, RMS_EPS, ALU.mult, ALU.add)\
                    .then_inc(ms_set, 1)

            def head_norm(s):
                dve.wait_ge(rms_set, s.upto(0))
                if s.began(0, 1):
                    dve.wait_ge(own_set, s.upto(0, 1))
                nc.vector.tensor_tensor(qkn[:, :, :], qk1[s.par(0)][:, :, :],
                                        rms[:, :].unsqueeze(2).broadcast_to([T, 2 * H, DH]),
                                        ALU.mult).then_inc(qkn_set, 1)

            def rotate(s):
                if not s.began(0, 1):
                    dve.wait_ge(rope_set, 1)
                dve.wait_ge(qkn_set, s.upto(0))
                if s.began(0, 1):
                    dve.wait_ge(qkr_set, s.upto(0, 1))
                for i in range(2):
                    dst = slice(i * HALF, (i + 1) * HALF)
                    src = slice((1 - i) * HALF, (2 - i) * HALF)
                    table = rope[:, DH + i * HALF:DH + (i + 1) * HALF].unsqueeze(1)
                    op = nc.vector.tensor_tensor(other[:, :, dst], qkn[:, :, src],
                                                 table.broadcast_to([T, 2 * H, HALF]), ALU.mult)
                op.then_inc(other_set, 1)

            def add_halves(s):
                dve.wait_ge(other_set, s.upto(0))
                dve.wait_ge(own_set, s.upto(0))
                if s.began(0, 1):
                    dve.wait_ge(high1_set, s.upto(0, 1))
                nc.vector.tensor_tensor(qkr[:, :, :], own[:, :, :], other[:, :, :], ALU.add)\
                    .then_inc(qkr_set, 1)

            def low_parts(slot, src):
                for i in range(2):
                    heads = slice(i * H, (i + 1) * H)
                    op = nc.vector.tensor_tensor(
                        slot[:, heads, (i + 1) * DH:(i + 2) * DH], src[:, heads, :],
                        slot[:, heads, 0:DH].bitcast(fp32), ALU.subtract)
                return op

            def low1(s):
                dve.wait_ge(high1_set, s.upto(0))
                low_parts(slot1, qkr[:, :, :]).then_inc(slot1_set, 1)

            def low2(s):
                dve.wait_ge(high2_set, s.upto(2))
                low_parts(slot2, ps_qk2.rearrange("t (h d) -> t h d", d=DH)).then_inc(slot2_set, 1)

            def residual1(s):
                dve.wait_ge(y1_done, s.upto(1))
                if s.began(1, 2):
                    dve.wait_ge(xc_set, s.upto(1, 2))
                if s.began(1, 2):
                    dve.wait_ge(h1b_set, s.upto(1, 2))
                nc.vector.tensor_tensor(h1[s.par(1)][:, :], ps_y1, h0[s.par(1)][:, :], ALU.add)\
                    .then_inc(h1_set, 1)

            def router_max(s):
                dve.wait_ge(gate_done, s.upto(2))
                nc.vector.tensor_reduce(nmax[:, :], ps_gate[:, R:R + E], AX.X, ALU.max, negate=True)\
                    .then_inc(nmax_set, 1)

            def route(s):
                dve.wait_ge(ex_set, s.upto(2))
                nc.vector.reciprocal(rsum[:, :], exsum[:, :]).then_inc(rsum_set, 1)
                nc.vector.max(top[:, :], ex[:, 0:E]).then_inc(top_set, 1)
                dve.wait_ge(top_set, s.upto(2))
                nc.vector.tensor_copy(top2[:, 0:2], top[:, 0:2]).then_inc(top2_set, 1)
                dve.wait_ge(rsum_set, s.upto(2))
                dve.wait_ge(top2_set, s.upto(2))
                nc.vector.tensor_scalar(lora_scale[:, :], rsum[:, :], LORA_SCALE, None, ALU.mult)\
                    .then_inc(scale_set, 1)
                nc.vector.match_replace(rest[:, :], top2[:, :], ex[:, :], 0.0).then_inc(rest_set, 1)
                dve.wait_ge(rest_set, s.upto(2))
                nc.vector.tensor_tensor(picked[:, :], ex[:, 0:E], rest[:, 0:E], ALU.subtract)\
                    .then_inc(picked_set, 1)
                dve.wait_ge(picked_set, s.upto(2))
                dve.wait_ge(scale_set, s.upto(2))
                dve.wait_ge(x2T_done, s.upto(2))
                nc.vector.tensor_scalar(xc[:, D + 1:D + 1 + E], picked[:, :], lora_scale[:, 0:1], None,
                                        ALU.mult).then_inc(combine_set, 1)
                dve.wait_ge(combine_set, s.upto(2))
                nc.vector.tensor_tensor(
                    hw[:, :, :], ps_gate[:, 0:R].rearrange("t (e r) -> t e r", e=E),
                    xc[:, D + 1:D + 1 + E].unsqueeze(2).broadcast_to([T, E, RANK]),
                    ALU.mult).then_inc(hw_set, 1)

            def shift(s, g):
                dve.wait_ge(s2_done[g], s.upto(3))
                heads = slice(g * HR, (g + 1) * HR)
                scores = ps_s2[g].rearrange("t (h k) -> t h k", h=HR)
                nc.vector.tensor_reduce(smax[:, heads], scores, AX.X, ALU.max).then_inc(smax_set[g], 1)
                dve.wait_ge(smax_set[g], s.upto(3))
                if s.began(3, 1):
                    dve.wait_ge(pT_done[g], s.upto(3, 1))
                nc.vector.tensor_tensor(prob[:, heads, :], scores,
                                        smax[:, heads].unsqueeze(2).broadcast_to([T, HR, T]),
                                        ALU.subtract).then_inc(shift_set[g], 1)

            def mask(s, g):
                dve.wait_ge(square_set[g], s.upto(1))
                heads = pat[:, g * HR:(g + 1) * HR, :]
                nc.vector.tensor_tensor(heads, heads, keep[:, :].unsqueeze(1).broadcast_to([T, HR, T]),
                                        ALU.mult).then_inc(pat_set[g], 1)

            def copy_probT(s, g):
                dve.wait_ge(pT_done[g], s.upto(3))
                if s.began(3, 1):
                    dve.wait_ge(zsT_done, s.upto(3, 1))
                nc.vector.tensor_copy(probT[:, g * HR:(g + 1) * HR, :],
                                      ps_pT[g].rearrange("t (h k) -> t h k", h=HR))\
                    .then_inc(pT_copied[g], 1)

            def divide(s):
                dve.wait_ge(zs_done, s.upto(4))
                z = ps_zs.rearrange("t (h d) -> t h d", d=VSLOT)
                nc.vector.reciprocal(rden[:, :], z[:, :, DH]).then_inc(rden_set, 1)
                dve.wait_ge(rden_set, s.upto(4))
                nc.vector.tensor_tensor(z2[:, :, :], z[:, :, 0:DH],
                                        rden[:, :].unsqueeze(2).broadcast_to([T, H, DH]),
                                        ALU.mult).then_inc(z2_set, 1)

            def residual2(s):
                dve.wait_ge(y2_done, s.upto(4))
                dve.wait_ge(h1b_set, s.upto(4))
                if s.began(4, 1):
                    dve.wait_ge(out_stored, s.upto(4, 1) * 16)
                nc.vector.tensor_tensor(out_sb[s.par(4)][:, :], ps_y2, h1b[s.par(4)][:, :], ALU.add)\
                    .then_inc(out_set, 1)

            def square_qk(s):
                dve.wait_ge(qk1_copied, s.upto(0))
                if s.began(0, 1):
                    dve.wait_ge(ss_set, s.upto(0, 1))
                q = qk1[s.par(0)][:, :, :]
                nc.vector.tensor_tensor(sq[:, :, :], q, q, ALU.mult).then_inc(sq_set, 1)

            def copy_z1T(s):
                dve.wait_ge(z1T_done, s.upto(1))
                nc.vector.tensor_copy(z1T[:, :, :], ps_z1T.rearrange("p (g t) -> p g t", g=VGROUPS)).then_inc(z1T_copied, 1)

            def step(s):
                s0, s1, s2, s3, s4 = (s.works(k) for k in range(STAGES))
                ahead = s.other(1)
                behind = s.other(-1)
                if behind.works(0): rotate(behind)
                if behind.works(1): moments1(behind)
                if behind.works(0): add_halves(behind)
                if s0: embed(s)
                if behind.works(1): normalize1(behind)
                if s0: stats0(s)
                if behind.works(0): low1(behind)
                if s0: moments0(s)
                if s3: shift(s, 0)
                if s2: router_max(s)
                if s0: normalize0(s)
                if s4: residual2(s)
                if s2: route(s)
                if s3: shift(s, 1); shift(s, 2)
                if s0: square_qk(s); head_sums(s)
                if s1: mask(s, 2)
                if s3: copy_probT(s, 1)
                if s1: mask(s, 1)
                if s3: copy_probT(s, 2)
                if s1: copy_z1T(s)
                if s2: low2(s)
                if s1: residual1(s)
                if ahead.works(4): divide(ahead)
                if s0: head_norm(s)
                if s1: stats1(s)

            dve.wait_ge(zeros_set, 10)
            nc.vector.memset(xn[:, D:D + 1], 1.0)
            nc.vector.memset(xc[:, D:D + 1], 1.0)
            nc.vector.memset(ex[:, E:2 * E], -1.0)
            nc.vector.memset(top2[:, :], -1.0)
            for i in range(2):
                nc.vector.memset(v2[i][:, :, DH:DH + 1], 1.0)
            dve.wait_ge(ident_in, 16 * 2)
            run(dve, step)

        @block.gpsimd
        def _(pool):
            def rstd0_(s):
                pool.wait_ge(var0_set, s.upto(0))
                if s.began(0, 1):
                    pool.wait_ge(xn_set, s.upto(0, 1))
                nc.gpsimd.tensor_tensor(rstd0[:, :], var0[:, :], minus_half[:, 0:1], ALU.pow)\
                    .then_inc(rstd0_set, 1)

            def rstd1_(s):
                pool.wait_ge(var1_set, s.upto(1))
                if s.began(1, 1):
                    pool.wait_ge(xc_set, s.upto(1, 1))
                nc.gpsimd.tensor_tensor(rstd1[:, :], var1[:, :], minus_half[:, 0:1], ALU.pow)\
                    .then_inc(rstd1_set, 1)

            def rms_(s):
                pool.wait_ge(ms_set, s.upto(0))
                if s.began(0, 1):
                    pool.wait_ge(qkn_set, s.upto(0, 1))
                nc.gpsimd.tensor_tensor(rms[:, :], ms[:, :], minus_half[:, :], ALU.pow)\
                    .then_inc(rms_set, 1)

            def own_half(s):
                pool.wait_ge(qkn_set, s.upto(0))
                if s.began(0, 1):
                    pool.wait_ge(qkr_set, s.upto(0, 1))
                nc.gpsimd.tensor_tensor(own[:, :, :], qkn[:, :, :],
                                        rope[:, 0:DH].unsqueeze(1).broadcast_to([T, 2 * H, DH]),
                                        ALU.mult).then_inc(own_set, 1)

            def mask(s, g):
                pool.wait_ge(square_set[g], s.upto(1))
                heads = pat[:, g * HR:(g + 1) * HR, :]
                nc.gpsimd.tensor_tensor(heads, heads, keep[:, :].unsqueeze(1).broadcast_to([T, HR, T]),
                                        ALU.mult).then_inc(pat_set[g], 1)

            def add_bias(s):
                if not s.began(2, 1):
                    pool.wait_ge(weights_in, 16 * WEIGHTS)
                pool.wait_ge(h1_set, s.upto(2))
                if s.began(2, 2):
                    pool.wait_ge(out_set, s.upto(2, 2))
                nc.gpsimd.tensor_tensor(h1b[s.par(2)][:, :], h1[s.par(2)][:, :], proj_b[:, :], ALU.add)\
                    .then_inc(h1b_set, 1)

            def step(s):
                s0, s1, s2, _, _ = (s.works(k) for k in range(STAGES))
                if s0: rstd0_(s)
                if s1: mask(s, 0)
                if s0: rms_(s)
                if s2: add_bias(s)
                if s0: own_half(s)
                if s1: rstd1_(s)

            for z in v1 + v2:
                nc.gpsimd.memset(z[:, :, :], 0.0).then_inc(zeros_set, 1)
            for z in (xn, xc):
                nc.gpsimd.memset(z[:, :], 0.0).then_inc(zeros_set, 1)
            nc.gpsimd.memset(slot1[:, :, :].bitcast(fp32), 0.0).then_inc(zeros_set, 1)
            nc.gpsimd.memset(minus_half[:, :], -0.5).then_inc(zeros_set, 1)
            for wide in (q1T, k2T):
                nc.gpsimd.memset(wide[:, :, :, :].bitcast(fp32), 0.0).then_inc(zeros_set, 1)
            pool.wait_ge(zeros_set, 10)
            pool.wait_ge(consts_in, 16 * CONSTS)
            nc.gpsimd.tensor_tensor(rope[:, :], rope_sb[:, :], g_sb[:, :], ALU.mult).then_inc(rope_set, 1)
            pool.wait_ge(rope_set, 1)
            run(pool, step)


def kernel(**inputs):
    import numpy as np
    import concourse.bacc as bacc
    from concourse.bass_utils import run_bass_kernel_spmd

    IMG, C, SIDE, PATCH, PER_TILE = 64, 3, 96, 16, 3
    H, DH, D, BASE = 12, 16, 192, 512.0
    N = SIDE // PATCH
    S = N * N
    TILES = -(-IMG // PER_TILE)
    T = PER_TILE * S

    x = np.asarray(inputs["x"])
    starts = [min(PER_TILE * t, IMG - PER_TILE) for t in range(TILES)]
    xt = x.reshape(IMG, C, N, PATCH, N, PATCH).transpose(1, 3, 5, 0, 2, 4).reshape(-1, 128, IMG, S)
    x_tiles = np.stack([xt[:, :, a:a + PER_TILE] for a in starts])
    x_tiles = x_tiles.transpose(0, 2, 1, 3, 4).reshape(TILES, 128, -1, T)

    g = {n: np.asarray(a) for n, a in inputs.items() if n != "x"}

    row = lambda n: g[n].reshape(1, -1)
    w_tok = g["L0_tok_W"].T.reshape(-1, 128, D).transpose(1, 0, 2)
    w_qkv1 = np.concatenate([np.concatenate([g["L0_attn_W" + c].T for c in "qkv"], 1),
                             np.concatenate([row("L0_attn_b" + c) for c in "qkv"], 1)], 0)
    a = g["L0_ffn_A"].reshape(-1, D)
    w_gate = np.concatenate([np.concatenate([a.T, g["L0_ffn_Wg"].T], 1),
                             np.concatenate([row("L0_ffn_ba"), row("L0_ffn_bg")], 1)], 0)
    w_qkv2 = np.concatenate([g["L0_ffn_Wqkv"].T, row("L0_ffn_bqkv"), g["L0_ffn_bb"]], 0)
    w_lora = g["L0_ffn_Bm"].transpose(0, 2, 1).reshape(-1, 3 * D)
    w_o1 = np.zeros((4, 32, H // 4, D), np.float32)
    w_o1[:, 0:DH] = g["L0_attn_Wo"].T.reshape(H // 4, 4, DH, D).transpose(1, 2, 0, 3)
    gain = g["L0_attn_g"]
    g_rows = np.concatenate([gain, gain[DH // 2:], gain[:DH // 2]]).reshape(1, -1)

    inv = (1.0 / BASE ** (np.arange(0, DH, 2, dtype=np.float32) / DH)).astype(np.float32)
    at = np.arange(T)
    freqs = np.outer((at % S).astype(np.float32), inv).astype(np.float32)
    cos, sin = np.cos(freqs), np.sin(freqs)
    rope_rows = np.concatenate([cos, cos, sin, -sin], 1).astype(np.float32)
    same = (at[:, None] // S) == (at[None, :] // S)
    causal_keep = (same & (at[:, None] <= at[None, :])).astype(np.float32)
    image = (at[:, None] // S == np.arange(PER_TILE)[None, :]).astype(np.float32)
    image_rows = np.zeros((T, 2, H, 64 - 3 * DH), np.float32)
    image_rows[:, 0, :, 0:PER_TILE] = image[:, None, :]
    image_rows[:, 1, :, 0:PER_TILE] = (1.0 - image[:, None, :]) * np.float32(-2.0 ** 99)
    identity = np.eye(128, dtype=np.float32)

    nc = bacc.Bacc("TRN2", target_bir_lowering=False, num_devices=1)
    arrays = dict(x_tiles=x_tiles, w_tok=w_tok, b_tok=row("L0_tok_b"), w_qkv1=w_qkv1,
                  w_o1=w_o1.reshape(128, H // 4, D), g_rows=g_rows, rope_rows=rope_rows,
                  causal_keep=causal_keep, w_gate=w_gate, w_qkv2=w_qkv2, w_lora=w_lora,
                  w_proj=g["L0_ffn_Wproj"].T, b_proj=row("L0_ffn_bproj"),
                  image_rows=image_rows, identity=identity)
    arrays = {n: np.ascontiguousarray(v) for n, v in arrays.items()}
    args = {n: nc.dram_tensor("in_" + n, v.shape, mybir.dt.from_np(v.dtype), kind="ExternalInput").ap()
            for n, v in arrays.items()}
    args["out"] = nc.dram_tensor("out_h", (TILES, T, D), mybir.dt.float32, kind="ExternalOutput").ap()
    vit_tower(nc, **args)
    r = run_bass_kernel_spmd(nc, [{"in_" + n: v for n, v in arrays.items()}], core_ids=[0])
    h = r.results[0]["out_h"].reshape(TILES, PER_TILE, S, D)
    own = PER_TILE * (TILES - 1) - starts[-1]
    return np.concatenate([h[:-1].reshape(-1, S, D), h[-1, own:]], 0)
```
